# Optimizing a Trainium2 kernel written in Bass

```python
import numpy as np
import jax
import jax.numpy as jnp

def _softmax(x, axis=-1):
    return jax.nn.softmax(x, axis=axis)

def _gelu(x):
    return jax.nn.gelu(x, approximate=True)

def _silu(x):
    return jax.nn.silu(x)

def _sigmoid(x):
    return jax.nn.sigmoid(x)

def _layernorm(x, axis=-1, eps=1e-05):
    m = jnp.mean(x, axis=axis, keepdims=True)
    v = jnp.var(x, axis=axis, keepdims=True)
    return (x - m) / jnp.sqrt(v + eps)

def _scatter_add(tgt, idx, src, axis=0):
    return tgt.at[idx].add(src)

def _segment_sum(src, seg, n):
    return jax.ops.segment_sum(src, seg, n)
kernel_name = 'mk_audio_tower_d1_tok_audfeat1024_r4_a91889'

def setup_inputs(seed: int=0):
    np.random.seed(seed)
    _w = jnp.asarray

    def _rec_inputs():
        import jax
        import jax.numpy as jnp
        _rk = jax.random.key(seed)
        x = 0.00021031 + 1.00007 * jax.random.normal(jax.random.fold_in(_rk, 1), (64, 125, 256), jnp.float32)
        return x
    x = _rec_inputs()

    def _L0_tok_setup():
        import jax, jax.numpy as jnp
        import numpy as np
        DB4_DEC_LO = np.array([-0.010597401784997278, 0.032883011666982945, 0.030841381835986965, -0.18703481171888114, -0.02798376941698385, 0.6308807679295904, 0.7148465705525415, 0.23037781330885523], dtype=np.float64)
        NUM_LEVELS = 2

        def _afb1d_low(y, h0):
            B, D, N = y.shape
            L = h0.shape[0]
            outsize = (N + L - 1) // 2
            p = 2 * (outsize - 1) - N + L
            yp = jnp.pad(y, ((0, 0), (0, 0), (p // 2, p - p // 2)))
            k = jnp.broadcast_to(h0[None, None, :], (D, 1, L))
            return jax.lax.conv_general_dilated(yp, k, window_strides=(2,), padding='VALID', dimension_numbers=('NCH', 'OIH', 'NCH'), feature_group_count=D)
        key = jax.random.key(seed)
        x = jax.random.normal(key, (8, 1024, 256), dtype=jnp.float32)
        h0 = jnp.asarray(DB4_DEC_LO[::-1].copy(), dtype=jnp.float32)
        return {'x': x, 'h0': h0}
    _L0_tok_all = _L0_tok_setup()
    _L0_tok_in = {k: v for k, v in _L0_tok_all.items() if k in ('h0',)}
    del _L0_tok_all

    def _L0_attn_setup():
        import jax, jax.numpy as jnp
        import numpy as np
        NUM_HEADS = 16
        ENCODER_DIM = 256
        HEAD_DIM = ENCODER_DIM // NUM_HEADS
        BATCH, SEQ_LEN = (2, 512)

        def alibi_slopes(num_heads):
            x = (2.0 ** 8) ** (1.0 / num_heads)
            return jnp.asarray([1.0 / x ** (i + 1) for i in range(num_heads)], dtype=jnp.float32)
        key = jax.random.key(seed)
        ks = jax.random.split(key, 9)
        d = ENCODER_DIM
        s = 0.02
        return {'inputs': jax.random.normal(ks[0], (BATCH, SEQ_LEN, d), dtype=jnp.float32), 'Wq': jax.random.normal(ks[1], (d, d), dtype=jnp.float32) * s, 'bq': jax.random.normal(ks[2], (d,), dtype=jnp.float32) * s, 'Wk': jax.random.normal(ks[3], (d, d), dtype=jnp.float32) * s, 'bk': jax.random.normal(ks[4], (d,), dtype=jnp.float32) * s, 'Wv': jax.random.normal(ks[5], (d, d), dtype=jnp.float32) * s, 'bv': jax.random.normal(ks[6], (d,), dtype=jnp.float32) * s, 'Wo': jax.random.normal(ks[7], (d, d), dtype=jnp.float32) * s, 'bo': jax.random.normal(ks[8], (d,), dtype=jnp.float32) * s}
    _L0_attn_all = _L0_attn_setup()
    _L0_attn_in = {k: v for k, v in _L0_attn_all.items() if k in ('Wq', 'bq', 'Wk', 'bk', 'Wv', 'bv', 'Wo', 'bo')}
    del _L0_attn_all

    def _L0_ffn_setup():
        import jax, jax.numpy as jnp
        import numpy as np
        B, S, D, H, E, K = (4, 512, 256, 1024, 8, 2)
        CAPACITY_FACTOR = 1.5
        C = int(CAPACITY_FACTOR * B * S * K / E)
        key = jax.random.key(seed)
        ks = jax.random.split(key, 6)
        x = jax.random.normal(ks[0], (B, S, D), dtype=jnp.float32)
        w_router = jax.random.normal(ks[1], (D, E), dtype=jnp.float32) * 0.02
        w1 = jax.random.normal(ks[2], (E, D, H), dtype=jnp.float32) * 0.02
        b1 = jnp.zeros((E, H), dtype=jnp.float32)
        w2 = jax.random.normal(ks[3], (E, H, D), dtype=jnp.float32) * 0.02
        b2 = jnp.zeros((E, D), dtype=jnp.float32)
        return {'x': x, 'w_router': w_router, 'w1': w1, 'b1': b1, 'w2': w2, 'b2': b2}
    _L0_ffn_all = _L0_ffn_setup()
    _L0_ffn_in = {k: v for k, v in _L0_ffn_all.items() if k in ('w_router', 'w1', 'b1', 'w2', 'b2')}
    del _L0_ffn_all
    return {'x': x, 'L0_tok_h0': _L0_tok_in['h0'], 'L0_attn_Wq': _L0_attn_in['Wq'], 'L0_attn_bq': _L0_attn_in['bq'], 'L0_attn_Wk': _L0_attn_in['Wk'], 'L0_attn_bk': _L0_attn_in['bk'], 'L0_attn_Wv': _L0_attn_in['Wv'], 'L0_attn_bv': _L0_attn_in['bv'], 'L0_attn_Wo': _L0_attn_in['Wo'], 'L0_attn_bo': _L0_attn_in['bo'], 'L0_ffn_w_router': _L0_ffn_in['w_router'], 'L0_ffn_w1': _L0_ffn_in['w1'], 'L0_ffn_b1': _L0_ffn_in['b1'], 'L0_ffn_w2': _L0_ffn_in['w2'], 'L0_ffn_b2': _L0_ffn_in['b2']}

def reference(x, L0_tok_h0, L0_attn_Wq, L0_attn_bq, L0_attn_Wk, L0_attn_bk, L0_attn_Wv, L0_attn_bv, L0_attn_Wo, L0_attn_bo, L0_ffn_w_router, L0_ffn_w1, L0_ffn_b1, L0_ffn_w2, L0_ffn_b2):
    import jax
    import jax.numpy as jnp

    def _L0_tok_ref(x, h0):
        import jax, jax.numpy as jnp
        import numpy as np
        DB4_DEC_LO = np.array([-0.010597401784997278, 0.032883011666982945, 0.030841381835986965, -0.18703481171888114, -0.02798376941698385, 0.6308807679295904, 0.7148465705525415, 0.23037781330885523], dtype=np.float64)
        NUM_LEVELS = 2

        def _afb1d_low(y, h0):
            B, D, N = y.shape
            L = h0.shape[0]
            outsize = (N + L - 1) // 2
            p = 2 * (outsize - 1) - N + L
            yp = jnp.pad(y, ((0, 0), (0, 0), (p // 2, p - p // 2)))
            k = jnp.broadcast_to(h0[None, None, :], (D, 1, L))
            return jax.lax.conv_general_dilated(yp, k, window_strides=(2,), padding='VALID', dimension_numbers=('NCH', 'OIH', 'NCH'), feature_group_count=D)
        y = jnp.swapaxes(x, 1, 2)
        for _ in range(NUM_LEVELS):
            y = _afb1d_low(y, h0)
        return jnp.swapaxes(y, 1, 2)

    def _L0_attn_ref(inputs, Wq, bq, Wk, bk, Wv, bv, Wo, bo):
        import jax, jax.numpy as jnp
        import numpy as np
        NUM_HEADS = 16
        ENCODER_DIM = 256
        HEAD_DIM = ENCODER_DIM // NUM_HEADS
        BATCH, SEQ_LEN = (2, 512)

        def alibi_slopes(num_heads):
            x = (2.0 ** 8) ** (1.0 / num_heads)
            return jnp.asarray([1.0 / x ** (i + 1) for i in range(num_heads)], dtype=jnp.float32)
        B, S, E = inputs.shape
        H, D = (NUM_HEADS, E // NUM_HEADS)

        def split_heads(x):
            return x.reshape(B, S, H, D).transpose(0, 2, 1, 3)
        q = split_heads(inputs @ Wq + bq)
        k = split_heads(inputs @ Wk + bk)
        v = split_heads(inputs @ Wv + bv)
        pos = jnp.arange(S)
        rel = (pos[None, :] - pos[None, :].T).astype(jnp.float32)
        bias = alibi_slopes(H)[:, None, None] * rel
        scale = 1.0 / jnp.sqrt(jnp.asarray(D, dtype=q.dtype))
        scores = jnp.einsum('bhqd,bhkd->bhqk', q, k) * scale + bias[None]
        attn = jax.nn.softmax(scores, axis=-1)
        ctx = jnp.einsum('bhqk,bhkd->bhqd', attn, v)
        ctx = ctx.transpose(0, 2, 1, 3).reshape(B, S, E)
        return ctx @ Wo + bo

    def _L0_ffn_ref(x, w_router, w1, b1, w2, b2):
        import jax, jax.numpy as jnp
        import numpy as np
        B, S, D, H, E, K = (4, 512, 256, 1024, 8, 2)
        CAPACITY_FACTOR = 1.5
        C = int(CAPACITY_FACTOR * B * S * K / E)
        Bs, Ss, Ds = x.shape
        N = Bs * Ss
        xf = x.reshape(N, Ds)
        logits = xf @ w_router
        probs = jax.nn.softmax(logits, axis=-1)
        gate, eidx = jax.lax.top_k(probs, K)
        gate = gate / jnp.sum(gate, axis=-1, keepdims=True)
        oh = jax.nn.one_hot(eidx, E, dtype=jnp.float32)
        ohf = oh.reshape(N * K, E)
        pos = jnp.cumsum(ohf, axis=0) - 1.0
        posk = jnp.sum(pos * ohf, axis=-1).reshape(N, K).astype(jnp.int32)
        keep = posk < C
        gate = gate * keep.astype(gate.dtype)
        e_flat = eidx.reshape(-1)
        p_flat = jnp.where(keep, posk, 0).reshape(-1)
        contrib = (xf[:, None, :] * keep[..., None].astype(xf.dtype)).reshape(N * K, Ds)
        expert_in = jnp.zeros((E, C, Ds), dtype=xf.dtype).at[e_flat, p_flat].add(contrib)
        h = jax.nn.relu(jnp.einsum('ecd,edh->ech', expert_in, w1) + b1[:, None, :])
        expert_out = jnp.einsum('ech,eho->eco', h, w2) + b2[:, None, :]
        tok = expert_out[e_flat, p_flat].reshape(N, K, -1)
        y = jnp.sum(tok * gate[..., None], axis=1)
        return y.reshape(Bs, Ss, -1)
    h = _L0_tok_ref(x, L0_tok_h0)
    h = h + _L0_attn_ref(_layernorm(h, axis=-1), L0_attn_Wq, L0_attn_bq, L0_attn_Wk, L0_attn_bk, L0_attn_Wv, L0_attn_bv, L0_attn_Wo, L0_attn_bo)
    h = h + _L0_ffn_ref(_layernorm(h, axis=-1), L0_ffn_w_router, L0_ffn_w1, L0_ffn_b1, L0_ffn_w2, L0_ffn_b2)
    return h

_drawn_inputs = setup_inputs


def setup_inputs(seed=0):
    import zlib

    import numpy as np

    out = dict(_drawn_inputs(seed))
    spreads = {'L0_ffn_b1': (0.0, 0.1), 'L0_ffn_b2': (0.0, 0.1)}
    factors = {'L0_attn_Wq': 6.198,
     'L0_attn_bq': 25.354,
     'L0_attn_Wk': 5.716,
     'L0_attn_bk': 64.0,
     'L0_attn_bv': 3.13}
    for name, (base, spread) in spreads.items():
        noise = np.random.default_rng([zlib.crc32(name.encode()), seed]).standard_normal(out[name].shape)
        drawn = base * np.exp(spread * noise) if base else spread * noise
        out[name] = jnp.asarray(drawn.astype(out[name].dtype))
    for name, factor in factors.items():
        out[name] = (out[name] * factor).astype(out[name].dtype)
    return out
```

```python
import concourse.bass as bass
from concourse import mybir
from contextlib import ExitStack

B, N_IN, D = 64, 125, 256
TAPS = 8
N_MID = (N_IN + TAPS - 1) // 2
T = (N_MID + TAPS - 1) // 2
PAD1 = (2 * (N_MID - 1) - N_IN + TAPS) // 2
PAD2 = (2 * (T - 1) - N_MID + TAPS) // 2
HEADS = 16
HD = D // HEADS
NB = 3
P = NB * T
GROUPS = -(-B // NB)
PAIRS = GROUPS // 2
LAST_BATCHES = B - NB * (GROUPS - 1)
QH = 4
QUADS = HEADS // QH
QW = QH * P
VW = HD + 1
KC = D // 128
E, K, HID = 8, 2, 1024
HC = HID // 128
TOKENS = B * T
CAP = int(1.5 * 4 * 512 * K / E)
TILE = 128
REGION = TOKENS + TILE
ROW = D + 2
SPILL = E * REGION
MAXT = TOKENS // TILE
PAD_ROW = GROUPS * P
OUT_ROWS = PAD_ROW + TILE
EPS = 1e-5
FAR = -1e30


def audio_tower(nc, x, h0, wq, bq, wk, bk, wv, bv, wo, bo, w_router, w1, b1, w2, b2, out):
    fp32, f32r, i32, u32 = mybir.dt.float32, mybir.dt.float32r, mybir.dt.int32, mybir.dt.uint32
    ALU = mybir.AluOpType
    ACT = mybir.ActivationFunctionType
    X = mybir.AxisListType.X
    ds = bass.ds

    ctx = ExitStack()
    with ctx:
        def sb(name, shape, dt=fp32):
            return ctx.enter_context(nc.sbuf_tensor(name, shape, dt))

        def sem(name):
            return ctx.enter_context(nc.semaphore(name))

        def wait(eng, semaphore, value):
            if not (isinstance(value, int) and value <= 0):
                eng.wait_ge(semaphore, value)

        passed = sem("passed")

        def stand(eng):
            eng.sem_inc(passed, 1)

        dispatch = nc.dram_tensor("dispatch", (SPILL + K * TILE, ROW), fp32).ap()

        h0_bc = sb("h0_bc", [128, TAPS])
        vec_rows = sb("vec_rows", [128, 128])
        vec_cols = sb("vec_cols", [128, E * HC + 2 * KC])
        b1_cols = vec_cols[:, 0:E * HC]
        bq_cols = vec_cols[:, E * HC:E * HC + KC]
        bk_cols = vec_cols[:, E * HC + KC:E * HC + 2 * KC]
        bv_bc = sb("bv_bc", [P, D])
        bo_bc = sb("bo_bc", [P, D])
        b2_bc = sb("b2_bc", [128, E, D])
        wq_sb = sb("wq_sb", [128, KC, D])
        wk_sb = sb("wk_sb", [128, KC, D])
        wv_sb = sb("wv_sb", [128, KC, D])
        wo_sb = sb("wo_sb", [128, KC, D])
        wr_sb = sb("wr_sb", [128, KC, E])
        ident = sb("ident", [128, 128])
        before = sb("before", [P, P])
        ones = sb("ones", [P, 128])
        tap1_i = sb("tap1_i", [N_MID, N_IN], i32)
        tap2_i = sb("tap2_i", [N_MID, T], i32)
        tap1 = sb("tap1", [N_MID, N_IN])
        tap2 = sb("tap2", [N_MID, T])
        hit1 = sb("hit1", [N_MID, N_IN])
        hit2 = sb("hit2", [N_MID, T])
        level1 = sb("level1", [N_MID, N_IN])
        level2 = sb("level2", [N_MID, T])
        wave = sb("wave", [N_IN, NB, P])
        rel_i = sb("rel_i", [P, P], i32)
        rel = sb("rel", [P, P])
        score_bias = sb("score_bias", [P, HEADS, P])
        part_i = sb("part_i", [128, 1], i32)
        part = sb("part", [128, 1])
        odd_i = sb("odd_i", [128, 1], i32)
        odd = sb("odd", [128, 2])
        experts_i = sb("experts_i", [128, E], i32)
        experts = sb("experts", [128, E])
        region = sb("region", [128, E])
        steps_i = sb("steps_i", [128, MAXT], i32)
        steps = sb("steps", [128, MAXT])
        live = sb("live", [128, 1])
        spill = sb("spill", [128, K])
        pad_rows = sb("pad_rows", [128, ROW])
        eps = sb("eps", [P, 1])
        minus_half = sb("minus_half", [P, 1])

        x_sb = sb("x_sb", [N_IN, 2, NB * D])
        h_sb = sb("h_sb", [P, 2, D])
        hbo = sb("hbo", [P, 2, D])
        stats = sb("stats", [P, 6])
        mv = sb("mv", [P, 2])
        var_eps = sb("var_eps", [P, 1])
        rstd = sb("rstd", [P, 1])
        xn = sb("xn", [P, D])
        xT = sb("xT", [128, KC, P])
        qT = sb("qT", [128, 2, KC, P])
        kT = sb("kT", [128, 2, 2, KC, P])
        va = sb("va", [P, 2, HEADS, VW])
        sc = sb("sc", [P, 2, QH, P])
        mx = sb("mx", [P, 2, QH])
        sm = sb("sm", [P, 2, QH, P])
        pr = sb("pr", [P, 2, QH, P])
        prT = sb("prT", [P, 2, QH, P])
        rden = sb("rden", [P, HEADS])
        cx = sb("cx", [P, HEADS, HD])
        cxT = sb("cxT", [128, KC, P])
        h2 = sb("h2", [P, 2, D])
        stats2 = sb("stats2", [P, 6])
        mv2 = sb("mv2", [P, 2])
        var_eps2 = sb("var_eps2", [P, 1])
        rstd2 = sb("rstd2", [P, 1])
        rows = sb("rows", [P, 2, K, ROW])
        x2T = sb("x2T", [128, KC, P])
        lg = sb("lg", [P, E])
        top = sb("top", [P, 8])
        top_i = sb("top_i", [P, 8], u32)
        neg_top = sb("neg_top", [P, 1])
        choice = sb("choice", [P, K])
        hot = sb("hot", [P, K, E])
        hot_any = sb("hot_any", [P, E])
        gexp = sb("gexp", [P, K])
        gsum = sb("gsum", [P, 1])
        grec = sb("grec", [P, 1])
        gate = sb("gate", [P, K])
        count = sb("count", [128, E])
        pos_all = sb("pos_all", [P, E])
        pos_hot = sb("pos_hot", [P, K, E])
        pos = sb("pos", [P, K])
        keep = sb("keep", [P, K])
        dest_f = sb("dest_f", [P, K])
        dest = sb("dest", [P, 2, K], i32)
        token = sb("token", [128, 1])

        full = sb("full", [128, E, MAXT])
        ntiles = sb("ntiles", [128, E])
        first = sb("first", [128, E + 1])
        origin = sb("origin", [128, E])
        first_i = sb("first_i", [128, E + 1], i32)
        origin_i = sb("origin_i", [128, E], i32)
        pad_dest = sb("pad_dest", [128, E])
        pad_dest_i = sb("pad_dest_i", [128, E], i32)

        st1 = sb("st1", [128, KC, HID])
        st2 = sb("st2", [128, HC, D])
        w1h = sb("w1h", [128, 2, KC, HID], f32r)
        w1l = sb("w1l", [128, 2, KC, HID], f32r)
        w2h = sb("w2h", [128, 2, HC, D], f32r)
        w2l = sb("w2l", [128, 2, HC, D], f32r)
        xr = sb("xr", [128, ROW])
        meta_next = sb("meta_next", [128, 2])
        meta = sb("meta", [128, 2])
        xh = sb("xh", [128, KC, TILE], f32r)
        xl = sb("xl", [128, KC, TILE], f32r)
        hf = sb("hf", [128, HC, TILE])
        hh = sb("hh", [128, HC, TILE], f32r)
        hl = sb("hl", [128, HC, TILE], f32r)
        b1_cur = sb("b1_cur", [128, HC])
        b2_cur = sb("b2_cur", [128, D])
        yb = sb("yb", [128, D])
        y = sb("y", [128, D])
        y_dest = sb("y_dest", [128, 1], i32)

        banks = [ctx.enter_context(nc.psum_tensor(f"bank{i}", [128, 512], fp32)) for i in range(8)]
        ps_scores, ps_probT = banks[0:2], banks[2:4]
        ps_ctx, ps_qk, ps_xv, ps_tail = banks[4:8]
        ps_hidden, ps_y, ps_xT = banks[0:4], banks[4], banks[5]

        const_loaded, proj_loaded, b2_loaded = sem("const_loaded"), sem("proj_loaded"), sem("b2_loaded")
        x_loaded = [sem("x_loaded0"), sem("x_loaded1")]
        stage0_loaded, stage_loaded = sem("stage0_loaded"), sem("stage_loaded")
        iotas_made, masks_made, pool_order = sem("iotas_made"), sem("masks_made"), sem("pool_order")
        dve_order, bias_scaled, bias_masked = sem("dve_order"), sem("bias_scaled"), sem("bias_masked")
        levels_made, wave_mm, wave_made = sem("levels_made"), sem("wave_mm"), sem("wave_made")
        vec_mm, setup_done = sem("vec_mm"), sem("setup_done")
        h_mm, h_done, hbo_done = sem("h_mm"), sem("h_done"), sem("hbo_done")
        mv_done, rstd_done = sem("mv_done"), sem("rstd_done")
        xn_done, xT_mm, xT_done = sem("xn_done"), sem("xT_mm"), sem("xT_done")
        qk_mm, v_mm, qk_done, v_done = sem("qk_mm"), sem("v_mm"), sem("qk_done"), sem("v_done")
        s_mm, sc_done, mx_done, sm_done = sem("s_mm"), sem("sc_done"), sem("mx_done"), sem("sm_done")
        pr_done, prT_mm, prT_done, av_mm = sem("pr_done"), sem("prT_mm"), sem("prT_done"), sem("av_mm")
        cx_done = sem("cx_done")
        cxT_mm, cxT_done, wo_mm, h2_done = sem("cxT_mm"), sem("cxT_done"), sem("wo_mm"), sem("h2_done")
        mv2_done, rstd2_done = sem("mv2_done"), sem("rstd2_done")
        h2_stored = [sem("h2_stored0"), sem("h2_stored1")]
        row0_done, row1_done, x2T_mm, x2T_done = sem("row0_done"), sem("row1_done"), sem("x2T_mm"), sem("x2T_done")
        lg_mm, top_done, hot_done, rank_mm = sem("lg_mm"), sem("top_done"), sem("hot_done"), sem("rank_mm")
        gexp_done, rank_read, dest_done = sem("gexp_done"), sem("rank_read"), sem("dest_done")
        scattered = [sem("scattered0"), sem("scattered1")]
        tables_done, pads_scattered = sem("tables_done"), sem("pads_scattered")
        w1_split, w2_split = sem("w1_split"), sem("w2_split")
        xr_loaded, xr_mm, meta_taken, xh_done, xs_done = (
            sem("xr_loaded"), sem("xr_mm"), sem("meta_taken"), sem("xh_done"), sem("xs_done"))
        hid_mm, hf_done, hs_done, y_mm, y_read, y_ready, y_added = (
            sem("hid_mm"), sem("hf_done"), sem("hs_done"), sem("y_mm"), sem("y_read"), sem("y_ready"), sem("y_added"))
        y_free = sem("y_free")
        ONE = 1
        act_b1 = sem("act_b1")

        def head(q, i):
            return 8 * (i // 2) + 2 * q + i % 2

        def num(g):
            return 2 * g[0] + g[1]

        def after(g):
            return (g[0], 1) if g[1] == 0 else (g[0] + 1, 0)

        def ahead_of(g):
            return (g[0] - 1, 1) if g[1] == 0 else (g[0], 0)

        def over_groups(eng, step):
            for r in (0, 1):
                step((0, r), r == 1, True)
            with eng.Fori(1, PAIRS - 1) as pair:
                for r in (0, 1):
                    step((pair, r), True, True)
            for r in (0, 1):
                step((PAIRS - 1, r), True, r == 0)

        def is_last(g):
            return isinstance(g[0], int) and num(g) == GROUPS - 1

        def load_table(eng, table, index):
            return eng.value_load(table[0:1, ds(index, 1)] if not isinstance(index, int)
                                  else table[0:1, index:index + 1], min_val=0, max_val=E * REGION)

        block = ctx.enter_context(nc.Block())

        @block.sync
        def _(sp):
            sp.dma_start(h0_bc[:, :], h0.partition_broadcast(128)).then_inc(const_loaded, 16)
            x_v = x.rearrange("b n d -> n b d")

            def load_x(g):
                dst = x_sb[:, g[1], :].rearrange("n (b d) -> n b d", b=NB)
                if is_last(g):
                    sp.dma_start(dst[:, 0:LAST_BATCHES, :], x_v[:, B - LAST_BATCHES:B, :]).then_inc(x_loaded[g[1]], 16)
                    sp.dma_start(dst[:, LAST_BATCHES:NB, :], x_v[:, 0:NB - LAST_BATCHES, :]).then_inc(x_loaded[g[1]], 16)
                else:
                    sp.dma_start(dst, x_v[:, ds(NB * num(g), NB), :]).then_inc(x_loaded[g[1]], 16)

            load_x((0, 0))
            sp.dma_start(wq_sb[:, :, :], wq.rearrange("(c p) n -> p c n", p=128)).then_inc(proj_loaded, 16)
            sp.dma_start(wk_sb[:, :, :], wk.rearrange("(c p) n -> p c n", p=128)).then_inc(proj_loaded, 16)
            sp.dma_start(wv_sb[:, :, :], wv.rearrange("(c p) n -> p c n", p=128)).then_inc(proj_loaded, 16)
            load_x((0, 1))
            sp.dma_start(wo_sb[:, :, :], wo.rearrange("(c p) n -> p c n", p=128)).then_inc(proj_loaded, 16)
            sp.dma_start(wr_sb[:, :, :], w_router.rearrange("(c p) n -> p c n", p=128)).then_inc(proj_loaded, 16)
            sp.dma_start(st1[:, :, :], w1[0, :, :].rearrange("(c p) n -> p c n", p=128)).then_inc(stage0_loaded, 16)
            sp.dma_start(st2[:, :, :], w2[0, :, :].rearrange("(c p) n -> p c n", p=128)).then_inc(stage0_loaded, 16)
            sp.dma_start(b2_bc[:, :, :].rearrange("p e d -> p (e d)"),
                         b2.rearrange("e d -> (e d)").partition_broadcast(128)).then_inc(b2_loaded, 16)

            def store_h2(g):
                sp.wait_ge(h2_done, num(g) + 1)
                sp.dma_start(out[ds(P * num(g), P), :], h2[:, g[1], :]).then_inc(h2_stored[g[1]], 16)

            def step(g, earlier, later):
                if not (isinstance(g[0], int) and num(g) + 2 >= GROUPS):
                    sp.wait_ge(h_mm, num(g) + 1)
                    load_x((g[0] + 1, g[1]))
                if earlier:
                    store_h2(ahead_of(g))

            for r in (0, 1):
                step((0, r), r == 1, True)
            with sp.Fori(1, PAIRS - 2) as pair:
                for r in (0, 1):
                    step((pair, r), True, True)
            for i in (PAIRS - 2, PAIRS - 1):
                for r in (0, 1):
                    step((i, r), True, True)
            store_h2((PAIRS - 1, 1))

            sp.wait_ge(tables_done, 1)
            for r in (0, 1):
                sp.wait_ge(scattered[r], 16 * K * PAIRS)
            sp.wait_ge(pads_scattered, 16 * E)
            with sp.Fori(0, E) as e:
                origin_e = load_table(sp, origin_i, e)
                first_e = load_table(sp, first_i, e)
                last_e = load_table(sp, first_i, e + 1)
                with sp.Fori(first_e, last_e) as t:
                    sp.wait_ge(xr_mm, ONE + t)
                    sp.wait_ge(meta_taken, ONE + t)
                    row = nc.s_assert_within(
                        origin_e + TILE * t, 0, SPILL - TILE,
                        skip_runtime_bounds_check_because="a region holds every token and a tile of padding")
                    sp.dma_start(xr[:, :], dispatch[ds(row, TILE), :]).then_inc(xr_loaded, 16)
            total = load_table(sp, first_i, E)
            sp.wait_ge(xr_mm, ONE + total)
            sp.wait_ge(meta_taken, ONE + total)
            sp.dma_start(xr[:, :], dispatch[0:TILE, :]).then_inc(xr_loaded, 16)
            sp.wait_ge(y_added, 16 * total)
            stand(sp)

        @block.gpsimd
        def _(pool):
            pool.iota(tap1_i[:, :], pattern=[[1, N_IN]], base=PAD1, channel_multiplier=-2)
            pool.iota(tap2_i[:, :], pattern=[[-2, T]], base=PAD2, channel_multiplier=1).then_inc(iotas_made, 1)
            pool.memset(ident[:, :], 0.0).then_inc(pool_order, 1)
            pool.memset(wave[:, :, :], 0.0).then_inc(masks_made, 1)
            pool.wait_ge(pool_order, 1)
            pool.affine_select(out=ident[:, :], in_=ident[:, :], compare_op=ALU.not_equal, fill=1.0, base=0,
                               pattern=[[-1, 128]], channel_multiplier=1).then_inc(masks_made, 1)
            pool.iota(rel_i[:, :], pattern=[[1, P]], base=0, channel_multiplier=-1)
            pool.iota(part_i[:, :], pattern=[[0, 1]], base=0, channel_multiplier=1)
            pool.iota(experts_i[:, :], pattern=[[1, E]], base=0, channel_multiplier=0)
            pool.iota(steps_i[:, :], pattern=[[TILE, MAXT]], base=0, channel_multiplier=0).then_inc(iotas_made, 1)
            pool.memset(before[:, :], 1.0).then_inc(pool_order, 1)
            pool.memset(ones[:, :], 1.0)
            pool.memset(eps[:, :], EPS)
            pool.memset(minus_half[:, :], -0.5)
            pool.memset(va[:, :, :, :].rearrange("p a h v -> p (a h v)"), 1.0)
            pool.memset(pad_rows[:, :], 0.0).then_inc(masks_made, 1)
            pool.wait_ge(pool_order, 2)
            pool.affine_select(out=before[:, :], in_=before[:, :], compare_op=ALU.is_gt, fill=0.0, base=0,
                               pattern=[[1, P]], channel_multiplier=-1).then_inc(masks_made, 1)
            grid = score_bias[:, :, :].rearrange("p h (b k) -> p h b k", b=NB)
            pool.wait_ge(bias_scaled, 1)
            pool.affine_select(out=grid, in_=grid, compare_op=ALU.is_ge, fill=FAR, base=0,
                               pattern=[[0, HEADS], [-T, NB], [0, T]], channel_multiplier=1).then_inc(pool_order, 1)
            pool.wait_ge(pool_order, 3)
            pool.affine_select(out=grid, in_=grid, compare_op=ALU.is_ge, fill=FAR, base=T - 1,
                               pattern=[[0, HEADS], [T, NB], [0, T]], channel_multiplier=-1).then_inc(bias_masked, 1)

            def bias_rows(g):
                n = num(g)
                pool.wait_ge(h_done, n + 1)
                wait(pool, h2_done, n - 1)
                pool.tensor_tensor(hbo[:, g[1], :], h_sb[:, g[1], :], bo_bc[:, :], ALU.add).then_inc(hbo_done, 1)

            def root(g, of, m, v, r, var_ready, ready):
                pool.wait_ge(var_ready, num(g) + 1)
                pool.tensor_tensor(v[:, :], m[:, 1:2], eps[:, :], ALU.add).then_inc(of, 1)
                pool.wait_ge(of, num(g) + 1)
                pool.tensor_tensor(r[:, :], v[:, :], minus_half[:, :], ALU.pow).then_inc(ready, 1)

            var1, var2 = sem("var1"), sem("var2")

            def root1(g):
                root(g, var1, mv, var_eps, rstd, mv_done, rstd_done)

            def root2(g):
                root(g, var2, mv2, var_eps2, rstd2, mv2_done, rstd2_done)

            root1((0, 0))
            pool.wait_ge(const_loaded, 16 * 6)
            bias_rows((0, 0))

            def split(slot, e):
                if isinstance(e, int) and e == 0:
                    pool.wait_ge(stage0_loaded, 32)
                else:
                    pool.wait_ge(stage_loaded, 32 * e)
                stand(pool)
                pool.tensor_copy(w1h[:, slot, :, :], st1[:, :, :]).then_inc(pool_order, 1)
                pool.tensor_copy(w2h[:, slot, :, :], st2[:, :, :]).then_inc(pool_order, 1)
                pool.wait_ge(pool_order, 3 + 2 * e + 1)
                pool.tensor_tensor(w1l[:, slot, :, :], st1[:, :, :], w1h[:, slot, :, :].bitcast(fp32),
                                   ALU.subtract).then_inc(w1_split, 1)
                pool.wait_ge(pool_order, 3 + 2 * e + 2)
                pool.tensor_tensor(w2l[:, slot, :, :], st2[:, :, :], w2h[:, slot, :, :].bitcast(fp32),
                                   ALU.subtract).then_inc(w2_split, 1)

            def stage(e):
                pool.wait_ge(w1_split, e)
                stand(pool)
                pool.dma_start(st1[:, :, :], w1[ds(e, 1), :, :].rearrange("e (c p) n -> p (e c) n", p=128))\
                    .then_inc(stage_loaded, 16)
                pool.wait_ge(w2_split, e)
                stand(pool)
                pool.dma_start(st2[:, :, :], w2[ds(e, 1), :, :].rearrange("e (c p) n -> p (e c) n", p=128))\
                    .then_inc(stage_loaded, 16)

            split(0, 0)
            stage(1)

            def less_max(g, q):
                n = QUADS * num(g) + q
                pool.wait_ge(mx_done, n + 1)
                wait(pool, pr_done, n - 1)
                pool.tensor_tensor(sm[:, q % 2, :, :], sc[:, q % 2, :, :],
                                   mx[:, q % 2, :].unsqueeze(2).broadcast_to([P, QH, P]), ALU.subtract)\
                    .then_inc(sm_done, 1)

            def second_row(g):
                pool.wait_ge(row0_done, num(g) + 1)
                stand(pool)
                pool.tensor_copy(rows[:, g[1], 1, 0:D], rows[:, g[1], 0, 0:D]).then_inc(row1_done, 1)

            def scatter(g):
                pool.wait_ge(dest_done, num(g) + 1)
                pool.wait_ge(row1_done, num(g) + 1)
                stand(pool)
                for k in range(K):
                    pool.indirect_dma_start(dispatch, bass.IndirectOffsetOnAxis(ap=dest[:, g[1], k:k + 1], axis=0),
                                            rows[:, g[1], k, :], None).then_inc(scattered[g[1]], 16)

            def step(g, earlier, later):
                less_max(g, 0)
                less_max(g, 1)
                less_max(g, 2)
                if earlier:
                    root2(ahead_of(g))
                if later:
                    root1(after(g))
                    bias_rows(after(g))
                if earlier:
                    second_row(ahead_of(g))
                less_max(g, 3)
                if earlier:
                    scatter(ahead_of(g))

            over_groups(pool, step)
            root2((PAIRS - 1, 1))
            second_row((PAIRS - 1, 1))
            scatter((PAIRS - 1, 1))

            pool.wait_ge(tables_done, 1)
            for e in range(E):
                pool.indirect_dma_start(dispatch, bass.IndirectOffsetOnAxis(ap=pad_dest_i[:, e:e + 1], axis=0),
                                        pad_rows[:, :], None).then_inc(pads_scattered, 16)

            pool.sem_inc(y_free, ONE)
            for r in (0, 1):
                pool.wait_ge(h2_stored[r], 16 * PAIRS)

            def tiles(e):
                first_e = load_table(pool, first_i, e)
                last_e = load_table(pool, first_i, e + 1)
                with pool.Fori(first_e, last_e) as t:
                    pool.wait_ge(y_ready, ONE + t + 1)
                    stand(pool)
                    pool.indirect_dma_start(out, bass.IndirectOffsetOnAxis(ap=y_dest[:, 0:1], axis=0), y[:, :], None,
                                            compute_op=ALU.add).then_inc(y_added, 16)
                    pool.wait_ge(y_added, 16 * t + 16)
                    pool.sem_inc(y_free, 1)

            def split_next(e, slot):
                pool.wait_ge(y_mm, ONE + load_table(pool, first_i, e))
                split(slot, e + 1)

            with pool.Fori(0, E // 2 - 1) as pair:
                for r in (0, 1):
                    e = 2 * pair + r
                    split_next(e, 1 - r)
                    stage(e + 2)
                    tiles(e)
            split_next(E - 2, 1)
            tiles(E - 2)
            tiles(E - 1)

        @block.scalar
        def _(act):
            act.dma_start(vec_rows[0:E * HC, :], b1.rearrange("e (j p) -> (e j) p", p=128)).then_inc(const_loaded, 16)
            act.dma_start(vec_rows[E * HC:E * HC + KC, :], bq.rearrange("(c p) -> c p", p=128)).then_inc(const_loaded, 16)
            act.dma_start(vec_rows[E * HC + KC:E * HC + 2 * KC, :], bk.rearrange("(c p) -> c p", p=128))\
                .then_inc(const_loaded, 16)
            act.dma_start(bv_bc[:, :], bv.partition_broadcast(P)).then_inc(const_loaded, 16)
            act.dma_start(bo_bc[:, :], bo.partition_broadcast(P)).then_inc(const_loaded, 16)

            def h_out(g):
                n = num(g)
                act.wait_ge(h_mm, n + 1)
                wait(act, hbo_done, n - 1)
                wait(act, xn_done, n - 1)
                act.activation(h_sb[:, g[1], :], ps_qk[0:P, 0:D], ACT.Copy).then_inc(h_done, 1)

            def xT_out(g):
                act.wait_ge(xT_mm, num(g) + 1)
                act.activation(xT[:, :, :].rearrange("p c n -> p (c n)"), ps_xv[:, 0:KC * P], ACT.Copy)\
                    .then_inc(xT_done, 1)

            def exp(g, q):
                n = QUADS * num(g) + q
                act.wait_ge(sm_done, n + 1)
                wait(act, prT_mm, n - 1)
                act.activation(pr[:, q % 2, :, :], sm[:, q % 2, :, :], ACT.Exp).then_inc(pr_done, 1)

            def probT_out(g, q):
                n = QUADS * num(g) + q
                act.wait_ge(prT_mm, n + 1)
                wait(act, av_mm, n - 1)
                act.activation(prT[:, q % 2, :, :].rearrange("p h k -> p (h k)"), ps_probT[q % 2][0:P, 0:QW], ACT.Copy)\
                    .then_inc(prT_done, 1)

            def ctxT_out(g):
                act.wait_ge(cxT_mm, num(g) + 1)
                act.activation(cxT[:, :, :].rearrange("p c n -> p (c n)"), ps_tail[:, 0:KC * P], ACT.Copy)\
                    .then_inc(cxT_done, 1)

            def x2T_out(g):
                act.wait_ge(x2T_mm, num(g) + 1)
                act.activation(x2T[:, :, :].rearrange("p c n -> p (c n)"), ps_tail[:, 0:KC * P], ACT.Copy)\
                    .then_inc(x2T_done, 1)

            def gate_exp(g):
                act.wait_ge(top_done, num(g) + 1)
                act.activation(gexp[:, :], top[:, 0:K], ACT.Exp, bias=neg_top[:, 0:1],
                               accum_out=gsum[:, 0:1]).then_inc(gexp_done, 1)

            h_out((0, 0))
            xT_out((0, 0))

            def step(g, earlier, later):
                exp(g, 0)
                if earlier:
                    ctxT_out(ahead_of(g))
                probT_out(g, 0)
                exp(g, 1)
                if later:
                    h_out(after(g))
                probT_out(g, 1)
                exp(g, 2)
                if earlier:
                    x2T_out(ahead_of(g))
                probT_out(g, 2)
                if later:
                    xT_out(after(g))
                exp(g, 3)
                probT_out(g, 3)
                if earlier:
                    gate_exp(ahead_of(g))

            over_groups(act, step)
            g = (PAIRS - 1, 1)
            ctxT_out(g)
            x2T_out(g)
            gate_exp(g)

            act.wait_ge(tables_done, 1)

            def x_high(n):
                act.wait_ge(xr_mm, ONE + n)
                act.activation(xh[:, :, :].rearrange("p c n -> p (c n)"), ps_xT[:, 0:KC * TILE], ACT.Copy)\
                    .then_inc(xh_done, 1)

            act.sem_inc(hf_done, ONE)
            x_high(1)
            with act.Fori(0, E) as e:
                first_e = load_table(act, first_i, e)
                act.wait_ge(hf_done, ONE + 4 * first_e)
                act.activation(b1_cur[:, :], b1_cols[:, ds(HC * e, HC)], ACT.Copy).then_inc(act_b1, 1)
                act.wait_ge(act_b1, e + 1)
                last_e = load_table(act, first_i, e + 1)
                with act.Fori(first_e, last_e) as t:
                    for b in range(4):
                        act.wait_ge(hid_mm, 4 * t + b + 1)
                        for half in (0, 1):
                            j = 2 * b + half
                            last = act.activation(hf[:, j, :], ps_hidden[b][:, half * TILE:(half + 1) * TILE], ACT.Relu,
                                                  bias=b1_cur[:, j:j + 1])
                        last.then_inc(hf_done, 1)
                    x_high(t + 2)

        @block.vector
        def _(dve):
            done = [0]

            def link(ins):
                done[0] += 1
                ins.then_inc(dve_order, 1)
                dve.wait_ge(dve_order, done[0])

            dve.wait_ge(iotas_made, 1)
            dve.wait_ge(const_loaded, 16 * 6)
            dve.tensor_copy(tap1[:, :], tap1_i[:, :])
            link(dve.tensor_copy(tap2[:, :], tap2_i[:, :]))
            for tap in range(TAPS):
                for src, hit, level in ((tap1, hit1, level1), (tap2, hit2, level2)):
                    dst = level if tap == 0 else hit
                    last = dve.tensor_scalar(dst[:, :], src[:, :], float(tap), h0_bc[0:N_MID, tap:tap + 1],
                                             ALU.is_equal, ALU.mult)
                link(last)
                if tap:
                    dve.tensor_tensor(level1[:, :], level1[:, :], hit1[:, :], ALU.add)
                    link(dve.tensor_tensor(level2[:, :], level2[:, :], hit2[:, :], ALU.add))
            dve.sem_inc(levels_made, 1)
            dve.wait_ge(iotas_made, 2)
            dve.tensor_copy(rel[:, :], rel_i[:, :])
            dve.tensor_copy(part[:, :], part_i[:, :])
            dve.tensor_copy(experts[:, :], experts_i[:, :])
            dve.tensor_copy(steps[:, :], steps_i[:, :])
            link(dve.tensor_scalar(odd_i[:, :], part_i[:, :], HD.bit_length() - 1, 1,
                                   ALU.logical_shift_right, ALU.bitwise_and))
            link(dve.tensor_copy(odd[:, 1:2], odd_i[:, :]))
            dve.tensor_scalar(odd[:, 0:1], odd[:, 1:2], -1.0, 1.0, ALU.mult, ALU.add)
            root = (2.0 ** 8) ** (1.0 / HEADS)
            for q in range(QUADS):
                for i in range(QH):
                    last = dve.tensor_scalar(score_bias[:, QH * q + i, :], rel[:, :],
                                             1.0 / root ** (head(q, i) + 1), None, ALU.mult)
            last.then_inc(bias_scaled, 1)
            dve.tensor_scalar(region[:, :], experts[:, :], float(REGION), None, ALU.mult)
            dve.tensor_scalar(live[:, :], part[:, :], float(LAST_BATCHES * T), None, ALU.is_lt)
            for k in range(K):
                dve.tensor_scalar(spill[:, k:k + 1], part[:, :], float(SPILL + TILE * k), None, ALU.add)
            dve.wait_ge(masks_made, 3)
            dve.tensor_scalar(pad_rows[:, D:D + 1].bitcast(i32), part[:, :], float(PAD_ROW), None, ALU.add)
            dve.tensor_copy(token[:, :], part[:, :])
            link(dve.memset(count[:, :], 0.0))
            dve.wait_ge(wave_mm, 1)
            for b in range(NB):
                last = dve.tensor_copy(wave[:, b, b * T:(b + 1) * T], ps_qk[0:N_IN, 0:T])
            last.then_inc(wave_made, 1)
            dve.wait_ge(vec_mm, 1)
            link(dve.tensor_copy(vec_cols[:, :], ps_tail[:, 0:E * HC + 2 * KC]))
            dve.sem_inc(setup_done, 1)
            per_group = [0]
            FIRST_STEP, WHOLE = 2, 13
            before_steps = [0]

            def base(g):
                return before_steps[0] + FIRST_STEP - WHOLE + WHOLE * num(g)

            def glink(ins, g):
                per_group[0] += 1
                ins.then_inc(dve_order, 1)
                dve.wait_ge(dve_order, base(g) + per_group[0])

            def moments1(g, at):
                dve.wait_ge(h_done, num(g) + 1)
                glink(dve.bn_stats(stats[:, :], h_sb[:, g[1], :]), at)
                stand(dve)
                dve.bn_aggr(mv[:, :], stats[:, :]).then_inc(mv_done, 1)

            def norm1(g):
                dve.wait_ge(rstd_done, num(g) + 1)
                wait(dve, xT_mm, num(g))
                dve.tensor_scalar(xn[:, :], h_sb[:, g[1], :], mv[:, 0:1], rstd[:, 0:1], ALU.subtract, ALU.mult)\
                    .then_inc(xn_done, 1)

            def qkv_out(g):
                n = num(g)
                r = g[1]
                dve.wait_ge(qk_mm, n + 1)
                for c in range(KC):
                    dve.tensor_scalar(qT[:, r, c, :], ps_qk[:, c * P:(c + 1) * P], bq_cols[:, c:c + 1], float(HD) ** -0.5,
                                      ALU.add, ALU.mult)
                for c in range(KC):
                    for odd_head in (0, 1):
                        last = dve.tensor_scalar(kT[:, r, odd_head, c, :], ps_qk[:, (KC + c) * P:(KC + c + 1) * P],
                                                 bk_cols[:, c:c + 1], odd[:, odd_head:odd_head + 1], ALU.add, ALU.mult)
                last.then_inc(qk_done, 1)
                dve.wait_ge(v_mm, n + 1)
                dve.tensor_tensor(va[:, r, :, 0:HD], ps_xv[0:P, 0:D].rearrange("p (h d) -> p h d", h=HEADS),
                                  bv_bc[:, :].rearrange("p (h d) -> p h d", h=HEADS), ALU.add).then_inc(v_done, 1)

            def scores(g, q):
                n = QUADS * num(g) + q
                dve.wait_ge(s_mm, n + 1)
                wait(dve, sm_done, n - 1)
                dve.tensor_tensor(sc[:, q % 2, :, :].rearrange("p h k -> p (h k)"), ps_scores[q % 2][0:P, 0:QW],
                                  score_bias[:, QH * q:QH * q + QH, :].rearrange("p h k -> p (h k)"), ALU.add)\
                    .then_inc(sc_done, 1)
                dve.wait_ge(sc_done, n + 1)
                dve.tensor_reduce(mx[:, q % 2, :], sc[:, q % 2, :, :], X, ALU.max).then_inc(mx_done, 1)

            def ctx_out(g):
                n = num(g)
                dve.wait_ge(av_mm, QUADS * n + QUADS)
                cv = ps_ctx[0:P, 0:HEADS * VW].rearrange("p (h v) -> p h v", h=HEADS)
                glink(dve.reciprocal(rden[:, :], cv[:, :, HD]), g)
                wait(dve, cxT_mm, n)
                dve.tensor_tensor(cx[:, :, :], cv[:, :, 0:HD], rden[:, :].unsqueeze(2).broadcast_to([P, HEADS, HD]),
                                  ALU.mult).then_inc(cx_done, 1)

            def moments2(g, at):
                n = num(g)
                r = g[1]
                dve.wait_ge(wo_mm, n + 1)
                dve.wait_ge(hbo_done, n + 1)
                wait(dve, h2_stored[r], 16 * g[0])
                wait(dve, scattered[r], 16 * K * g[0])
                dve.tensor_tensor(h2[:, r, :], ps_tail[0:P, 0:D], hbo[:, r, :], ALU.add).then_inc(h2_done, 1)
                dve.wait_ge(h2_done, n + 1)
                glink(dve.bn_stats(stats2[:, :], h2[:, r, :]), at)
                stand(dve)
                dve.bn_aggr(mv2[:, :], stats2[:, :]).then_inc(mv2_done, 1)

            def norm2(g):
                dve.wait_ge(rstd2_done, num(g) + 1)
                dve.tensor_scalar(rows[:, g[1], 0, 0:D], h2[:, g[1], :], mv2[:, 0:1], rstd2[:, 0:1],
                                  ALU.subtract, ALU.mult).then_inc(row0_done, 1)

            def choose(g, at):
                n = num(g)
                dve.wait_ge(lg_mm, n + 1)
                glink(dve.tensor_copy(lg[:, :], ps_tail[0:P, 256:256 + E]), at)
                stand(dve)
                glink(dve.max(top[:, :], lg[:, :]), at)
                dve.tensor_scalar(neg_top[:, :], top[:, 0:1], -1.0, None, ALU.mult).then_inc(top_done, 1)
                if not (isinstance(g[0], int) and n == 0):
                    dve.tensor_scalar(token[:, :], token[:, :], float(P), None, ALU.add)
                glink(dve.max_index(top_i[:, :], top[:, :], lg[:, :]), at)
                glink(dve.tensor_copy(choice[:, :], top_i[:, 0:K]), at)
                glink(dve.tensor_tensor(hot[:, :, :], experts[0:P, :].unsqueeze(1).broadcast_to([P, K, E]),
                                        choice[:, :].unsqueeze(2).broadcast_to([P, K, E]), ALU.is_equal), at)
                if is_last(g):
                    link_last(dve.tensor_scalar(hot[:, :, :], hot[:, :, :], live[0:P, 0:1], None, ALU.mult))
                dve.tensor_tensor(hot_any[:, :], hot[:, 0, :], hot[:, 1, :], ALU.add).then_inc(hot_done, 1)

            last_links = [0]
            last_order = sem("last_order")

            def link_last(ins):
                last_links[0] += 1
                ins.then_inc(last_order, 1)
                dve.wait_ge(last_order, last_links[0])

            def place(g, at):
                n = num(g)
                r = g[1]
                dve.wait_ge(rank_mm, n + 1)
                glink(dve.tensor_tensor(pos_all[:, :], ps_tail[0:P, 264:264 + E], count[0:P, :], ALU.add), at)
                dve.tensor_tensor(count[:, :], ps_tail[:, 272:272 + E], count[:, :], ALU.add).then_inc(rank_read, 1)
                glink(dve.tensor_tensor(pos_hot[:, :, :], hot[:, :, :], pos_all[:, :].unsqueeze(1).broadcast_to([P, K, E]),
                                        ALU.mult), at)
                glink(dve.tensor_reduce(pos[:, :], pos_hot[:, :, :], X, ALU.add), at)
                dve.wait_ge(gexp_done, n + 1)
                dve.reciprocal(grec[:, :], gsum[:, :])
                dve.tensor_scalar(keep[:, :], pos[:, :], float(CAP), None, ALU.is_lt)
                glink(dve.scalar_tensor_tensor(dest_f[:, :], choice[:, :], float(REGION), pos[:, :], ALU.mult, ALU.add), at)
                if is_last(g):
                    link_last(dve.tensor_scalar(dest_f[:, :], dest_f[:, :], live[0:P, 0:1], None, ALU.mult))
                    link_last(dve.tensor_scalar(keep[:, :], keep[:, :], live[0:P, 0:1], None, ALU.mult))
                    dve.tensor_scalar(neg_top[:, :], live[0:P, :], -1.0, 1.0, ALU.mult, ALU.add)
                    link_last(dve.tensor_scalar(gate[:, :], spill[0:P, :], 1.0, None, ALU.mult))
                    link_last(dve.tensor_scalar(gate[:, :], gate[:, :], neg_top[:, 0:1], None, ALU.mult))
                    link_last(dve.tensor_tensor(dest_f[:, :], dest_f[:, :], gate[:, :], ALU.add))
                dve.tensor_copy(dest[:, r, :], dest_f[:, :])
                glink(dve.tensor_scalar(gate[:, :], gexp[:, :], grec[:, 0:1], None, ALU.mult), at)
                dve.tensor_tensor(rows[:, r, :, D + 1], gate[:, :], keep[:, :], ALU.mult)
                for k in range(K):
                    last = dve.tensor_copy(rows[:, r, k, D:D + 1].bitcast(i32), token[0:P, :])
                last.then_inc(dest_done, 1)

            def norm1_first():
                g = (0, 0)
                dve.wait_ge(h_done, 1)
                link(dve.bn_stats(stats[:, :], h_sb[:, 0, :]))
                dve.bn_aggr(mv[:, :], stats[:, :]).then_inc(mv_done, 1)
                norm1(g)
                qkv_out(g)

            norm1_first()
            before_steps[0] = done[0]

            def step(g, earlier, later):
                per_group[0] = 0 if earlier else WHOLE - FIRST_STEP
                scores(g, 0)
                scores(g, 1)
                scores(g, 2)
                if earlier:
                    moments2(ahead_of(g), g)
                if later:
                    moments1(after(g), g)
                if earlier:
                    norm2(ahead_of(g))
                if later:
                    norm1(after(g))
                scores(g, 3)
                if earlier:
                    choose(ahead_of(g), g)
                if later:
                    qkv_out(after(g))
                ctx_out(g)
                if earlier:
                    place(ahead_of(g), g)

            over_groups(dve, step)
            g, at = (PAIRS - 1, 1), (PAIRS, 0)
            per_group[0] = -1
            moments2(g, at)
            norm2(g)
            choose(g, at)
            place(g, at)
            done[0] = base(at) + per_group[0]

            dve.wait_ge(rank_read, GROUPS)
            dve.tensor_tensor(pad_dest[:, :], count[:, :], region[:, :], ALU.add)
            link(dve.tensor_tensor(full[:, :, :], count[:, :].unsqueeze(2).broadcast_to([128, E, MAXT]),
                                   steps[:, :].unsqueeze(1).broadcast_to([128, E, MAXT]), ALU.is_gt))
            dve.tensor_scalar(pad_dest_i[:, :], pad_dest[:, :], part[:, 0:1], None, ALU.add)
            link(dve.tensor_reduce(ntiles[:, :], full[:, :, :], X, ALU.add))
            dve.memset(first[:, 0:1], 0.0)
            link(dve.tensor_scalar(ntiles[:, :], ntiles[:, :], 1.0, None, ALU.max))
            for e in range(E):
                link(dve.tensor_tensor(first[:, e + 1:e + 2], first[:, e:e + 1], ntiles[:, e:e + 1], ALU.add))
            dve.tensor_copy(first_i[:, :], first[:, :])
            link(dve.scalar_tensor_tensor(origin[:, :], first[:, 0:E], -float(TILE), region[:, :], ALU.mult, ALU.add))
            link(dve.tensor_copy(origin_i[:, :], origin[:, :]))
            dve.sem_inc(tables_done, 1)

            def x_low(t):
                dve.wait_ge(xr_loaded, 16 * (t + 1))
                dve.tensor_copy(meta_next[:, :], xr[:, D:ROW]).then_inc(meta_taken, 1)
                dve.wait_ge(xh_done, t + 1)
                dve.tensor_tensor(xl[:, :, :].rearrange("p c n -> p (c n)"), ps_xT[:, 0:KC * TILE],
                                  xh[:, :, :].bitcast(fp32).rearrange("p c n -> p (c n)"), ALU.subtract).then_inc(xs_done, 1)

            hid_high, out_biased = sem("hid_high"), sem("out_biased")
            for s in (meta_taken, y_read, y_ready):
                dve.sem_inc(s, ONE)
            x_low(0)
            dve.wait_ge(b2_loaded, 16)
            with dve.Fori(0, E) as e:
                first_e = load_table(dve, first_i, e)
                dve.wait_ge(y_read, ONE + first_e)
                dve.tensor_copy(b2_cur[:, :], b2_bc[:, ds(e, 1), :].rearrange("p e d -> p (e d)"))
                last_e = load_table(dve, first_i, e + 1)
                with dve.Fori(first_e, last_e) as t:
                    dve.wait_ge(y_ready, ONE + t)
                    dve.wait_ge(meta_taken, ONE + t + 1)
                    dve.tensor_copy(meta[:, :], meta_next[:, :])
                    for b in range(4):
                        dve.wait_ge(hf_done, ONE + 4 * t + b + 1)
                        dve.tensor_copy(hh[:, 2 * b:2 * b + 2, :], hf[:, 2 * b:2 * b + 2, :]).then_inc(hid_high, 1)
                        dve.wait_ge(hid_high, 4 * t + b + 1)
                        dve.tensor_tensor(hl[:, 2 * b:2 * b + 2, :], hf[:, 2 * b:2 * b + 2, :],
                                          hh[:, 2 * b:2 * b + 2, :].bitcast(fp32), ALU.subtract).then_inc(hs_done, 1)
                    x_low(t + 1)
                    dve.wait_ge(y_mm, ONE + t + 1)
                    dve.tensor_tensor(yb[:, :], ps_y[:, 0:D], b2_cur[:, :], ALU.add).then_inc(y_read, 1)
                    dve.wait_ge(y_free, ONE + t)
                    dve.wait_ge(y_read, ONE + t + 1)
                    dve.tensor_copy(y_dest[:, :], meta[:, 0:1].bitcast(i32))
                    dve.tensor_scalar(y[:, :], yb[:, :], meta[:, 1:2], None, ALU.mult).then_inc(y_ready, 1)

        @block.tensor
        def _(pe):
            def transposes(dst, src, rows_, cols):
                for c in range(KC):
                    last = pe.transpose(dst[:, c * cols:(c + 1) * cols], src[:, c * 128:(c + 1) * 128],
                                        ident[0:rows_, 0:rows_])
                return last

            pe.wait_ge(levels_made, 1)
            pe.matmul(ps_qk[0:N_IN, 0:T], level1[:, :], level2[:, :], start=True, stop=True).then_inc(wave_mm, 1)
            pe.wait_ge(masks_made, 4)
            pe.wait_ge(const_loaded, 16 * 6)
            n_vec = E * HC + 2 * KC
            pe.transpose(ps_tail[:, 0:n_vec], vec_rows[0:n_vec, :], ident[0:n_vec, 0:n_vec]).then_inc(vec_mm, 1)
            pe.wait_ge(wave_made, 1)

            def wavelet(g):
                r = g[1]
                pe.wait_ge(x_loaded[r], 16 * g[0] + (32 if is_last(g) else 16))
                wait(pe, qk_done, num(g))
                for b in range(NB):
                    last = pe.matmul(ps_qk[0:P, 0:D], wave[:, b, :], x_sb[:, r, b * D:(b + 1) * D],
                                     start=(b == 0), stop=(b == NB - 1))
                last.then_inc(h_mm, 1)

            def norm_T(g):
                pe.wait_ge(xn_done, num(g) + 1)
                wait(pe, v_done, num(g))
                transposes(ps_xv, xn, P, P).then_inc(xT_mm, 1)

            def qkv(g):
                pe.wait_ge(xT_done, num(g) + 1)
                for i, w in enumerate((wq_sb, wk_sb)):
                    for m in range(KC):
                        for c in range(KC):
                            last = pe.matmul(ps_qk[:, (KC * i + m) * P:(KC * i + m + 1) * P],
                                             w[:, c, m * 128:(m + 1) * 128], xT[:, c, :], start=(c == 0), stop=(c == KC - 1))
                last.then_inc(qk_mm, 1)
                for c in range(KC):
                    last = pe.matmul(ps_xv[0:P, 0:D], xT[:, c, :], wv_sb[:, c, :], start=(c == 0), stop=(c == KC - 1))
                last.then_inc(v_mm, 1)

            def scores(g, q):
                n = QUADS * num(g) + q
                if q == 0:
                    pe.wait_ge(qk_done, num(g) + 1)
                wait(pe, sc_done, n - 1)
                at = slice(32 * q, 32 * q + 32)
                for i in range(QH):
                    c, odd_head = i // 2, i % 2
                    last = pe.matmul(ps_scores[q % 2][0:P, i * P:(i + 1) * P], qT[at, g[1], c, :],
                                     kT[at, g[1], odd_head, c, :], start=True, stop=True)
                last.then_inc(s_mm, 1)

            def prob_T(g, q):
                n = QUADS * num(g) + q
                pe.wait_ge(pr_done, n + 1)
                wait(pe, prT_done, n - 1)
                for i in range(QH):
                    last = pe.transpose(ps_probT[q % 2][0:P, i * P:(i + 1) * P], pr[:, q % 2, i, :], ident[0:P, 0:P])
                last.then_inc(prT_mm, 1)

            def values(g, q):
                n = QUADS * num(g) + q
                pe.wait_ge(prT_done, n + 1)
                if q == 0:
                    pe.wait_ge(v_done, num(g) + 1)
                    wait(pe, cx_done, num(g))
                for i in range(QH):
                    h = head(q, i)
                    last = pe.matmul(ps_ctx[0:P, h * VW:(h + 1) * VW], prT[:, q % 2, i, :], va[:, g[1], h, :],
                                     start=True, stop=True)
                last.then_inc(av_mm, 1)

            def ctx_T(g):
                pe.wait_ge(cx_done, num(g) + 1)
                wait(pe, rank_read, num(g))
                transposes(ps_tail, cx[:, :, :].rearrange("p h d -> p (h d)"), P, P).then_inc(cxT_mm, 1)

            def project(g):
                pe.wait_ge(cxT_done, num(g) + 1)
                for c in range(KC):
                    last = pe.matmul(ps_tail[0:P, 0:D], cxT[:, c, :], wo_sb[:, c, :], start=(c == 0), stop=(c == KC - 1))
                last.then_inc(wo_mm, 1)

            def norm2_T(g):
                pe.wait_ge(row0_done, num(g) + 1)
                transposes(ps_tail, rows[:, g[1], 0, :], P, P).then_inc(x2T_mm, 1)

            def route(g):
                pe.wait_ge(x2T_done, num(g) + 1)
                for c in range(KC):
                    last = pe.matmul(ps_tail[0:P, 256:256 + E], x2T[:, c, :], wr_sb[:, c, :], start=(c == 0), stop=(c == KC - 1))
                last.then_inc(lg_mm, 1)

            def rank(g):
                pe.wait_ge(hot_done, num(g) + 1)
                pe.matmul(ps_tail[0:P, 264:264 + E], before[:, :], hot_any[:, :], start=True, stop=True)
                pe.matmul(ps_tail[:, 272:272 + E], ones[:, :], hot_any[:, :], start=True, stop=True).then_inc(rank_mm, 1)

            pe.wait_ge(proj_loaded, 16 * 5)
            wavelet((0, 0))
            norm_T((0, 0))
            pe.wait_ge(setup_done, 1)
            qkv((0, 0))
            pe.wait_ge(bias_masked, 1)

            def step(g, earlier, later):
                scores(g, 0)
                scores(g, 1)
                if earlier:
                    ctx_T(ahead_of(g))
                prob_T(g, 0)
                scores(g, 2)
                values(g, 0)
                if earlier:
                    project(ahead_of(g))
                if later:
                    wavelet(after(g))
                prob_T(g, 1)
                scores(g, 3)
                values(g, 1)
                if earlier:
                    norm2_T(ahead_of(g))
                prob_T(g, 2)
                if later:
                    norm_T(after(g))
                values(g, 2)
                if earlier:
                    route(ahead_of(g))
                prob_T(g, 3)
                if later:
                    qkv(after(g))
                values(g, 3)
                if earlier:
                    rank(ahead_of(g))

            over_groups(pe, step)
            g = (PAIRS - 1, 1)
            ctx_T(g)
            project(g)
            norm2_T(g)
            route(g)
            rank(g)

            pe.wait_ge(tables_done, 1)

            def row_T(n):
                pe.wait_ge(xr_loaded, 16 * n)
                transposes(ps_xT, xr, TILE, TILE).then_inc(xr_mm, 1)

            for s in (xr_mm, y_mm):
                pe.sem_inc(s, ONE)
            row_T(1)
            with pe.Fori(0, E // 2) as pair:
                for slot in (0, 1):
                    e = 2 * pair + slot
                    pe.wait_ge(w1_split, e + 1)
                    pe.wait_ge(w2_split, e + 1)
                    stand(pe)
                    first_e = load_table(pe, first_i, e)
                    last_e = load_table(pe, first_i, e + 1)
                    with pe.Fori(first_e, last_e) as t:
                        pe.wait_ge(xs_done, t + 1)
                        for b in range(4):
                            for half in (0, 1):
                                j = 2 * b + half
                                js = slice(j * 128, (j + 1) * 128)
                                terms = [(w, v, c) for c in range(KC)
                                         for w, v in ((w1h, xh), (w1h, xl), (w1l, xh))]
                                for i, (w, v, c) in enumerate(terms):
                                    last = pe.matmul(ps_hidden[b][:, half * TILE:(half + 1) * TILE], w[:, slot, c, js],
                                                     v[:, c, :], start=(i == 0), stop=(i == len(terms) - 1))
                            last.then_inc(hid_mm, 1)
                        row_T(t + 2)
                        pe.wait_ge(y_read, ONE + t)
                        for j in range(HC):
                            if j % 2 == 0:
                                pe.wait_ge(hs_done, 4 * t + j // 2 + 1)
                            for i, (v, w) in enumerate(((hh, w2h), (hh, w2l), (hl, w2h))):
                                last = pe.matmul(ps_y[:, 0:D], v[:, j, :], w[:, slot, j, :],
                                                 start=(j == 0 and i == 0), stop=(j == HC - 1 and i == 2))
                        last.then_inc(y_mm, 1)


_INS = ['x', 'L0_tok_h0', 'L0_attn_Wq', 'L0_attn_bq', 'L0_attn_Wk', 'L0_attn_bk', 'L0_attn_Wv', 'L0_attn_bv',
        'L0_attn_Wo', 'L0_attn_bo', 'L0_ffn_w_router', 'L0_ffn_w1', 'L0_ffn_b1', 'L0_ffn_w2', 'L0_ffn_b2']


def kernel(**inputs):
    import numpy as _np
    import concourse.bacc as _bacc
    from concourse import mybir as _mybir
    from concourse.bass_utils import run_bass_kernel_spmd as _run

    nc = _bacc.Bacc("TRN2", target_bir_lowering=False, num_devices=1)
    arrays, args = {}, []
    for name in _INS:
        a = _np.ascontiguousarray(inputs[name])
        arrays[f"in_{name}"] = a
        args.append(nc.dram_tensor(f"in_{name}", a.shape, _mybir.dt.from_np(a.dtype), kind="ExternalInput").ap())
    args.append(nc.dram_tensor("out_rows", (OUT_ROWS, D), _mybir.dt.float32, kind="ExternalOutput").ap())
    audio_tower(nc, *args)
    r = _run(nc, [arrays], core_ids=[0])
    return _np.asarray(r.results[0]["out_rows"])[0:TOKENS].reshape(B, T, D)
```

```python
import concourse.bass as bass
from concourse import mybir
from contextlib import ExitStack

B, N_IN, D = 64, 125, 256
TAPS = 8
N_MID = (N_IN + TAPS - 1) // 2
T = (N_MID + TAPS - 1) // 2
PAD1 = (2 * (N_MID - 1) - N_IN + TAPS) // 2
PAD2 = (2 * (T - 1) - N_MID + TAPS) // 2
HEADS = 16
HD = D // HEADS
NB = 3
P = NB * T
GROUPS = -(-B // NB)
PAIRS = GROUPS // 2
LAST_BATCHES = B - NB * (GROUPS - 1)
KC = D // 128
HB = HEADS // KC
QH = 4
QUADS = HEADS // QH
HPAIRS = HEADS // 2
E, K, HID = 8, 2, 1024
HC = HID // 128
TOKENS = B * T
CAP = int(1.5 * 4 * 512 * K / E)
HALF = 128
TILE = 2 * HALF
REGION = TOKENS + TILE
ROW = D + 2
SPILL = E * REGION
MAXT = -(-TOKENS // TILE)
PAD_ROW = GROUPS * P
OUT_ROWS = PAD_ROW + HALF
EPS = 1e-5


def audio_tower(nc, x, h0, wq, bq, wk, bk, wv, bv, wo, bo, w_router, w1, b1, w2, b2, out):
    fp32, f32r, i32, u32 = mybir.dt.float32, mybir.dt.float32r, mybir.dt.int32, mybir.dt.uint32
    ALU = mybir.AluOpType
    ACT = mybir.ActivationFunctionType
    X = mybir.AxisListType.X
    ds = bass.ds

    ctx = ExitStack()
    with ctx:
        def sb(name, shape, dt=fp32):
            return ctx.enter_context(nc.sbuf_tensor(name, shape, dt))

        def sem(name):
            return ctx.enter_context(nc.semaphore(name))

        def wait(eng, semaphore, value):
            if not (isinstance(value, int) and value <= 0):
                eng.wait_ge(semaphore, value)

        passed = sem("passed")

        def stand(eng):
            eng.sem_inc(passed, 1)

        dispatch = nc.dram_tensor("dispatch", (SPILL + K * HALF, ROW), fp32).ap()

        h0_bc = sb("h0_bc", [128, TAPS])
        vec_rows = sb("vec_rows", [128, 128])
        vec_cols = sb("vec_cols", [128, E * HC + 2 * KC])
        b1_cols = vec_cols[:, 0:E * HC]
        bq_cols = vec_cols[:, E * HC:E * HC + KC]
        bk_cols = vec_cols[:, E * HC + KC:E * HC + 2 * KC]
        bv_bc = sb("bv_bc", [P, D])
        bo_bc = sb("bo_bc", [P, D])
        b2_bc = sb("b2_bc", [128, E, D])
        wq_sb = sb("wq_sb", [128, KC, D])
        wk_sb = sb("wk_sb", [128, KC, D])
        wv_sb = sb("wv_sb", [128, KC, D])
        wo_sb = sb("wo_sb", [128, KC, D])
        wr_sb = sb("wr_sb", [128, KC, E])
        ident = sb("ident", [128, 128])
        before = sb("before", [P, P])
        ones = sb("ones", [P, 128])
        tap1_i = sb("tap1_i", [N_MID, N_IN], i32)
        tap2_i = sb("tap2_i", [N_MID, T], i32)
        tap1 = sb("tap1", [N_MID, N_IN])
        tap2 = sb("tap2", [N_MID, T])
        hit1 = sb("hit1", [N_MID, N_IN])
        hit2 = sb("hit2", [N_MID, T])
        level1 = sb("level1", [N_MID, N_IN])
        level2 = sb("level2", [N_MID, T])
        wave = sb("wave", [N_IN, NB, P])
        rel_i = sb("rel_i", [P, T], i32)
        rel = sb("rel", [P, T])
        reached = sb("reached", [P, NB + 1])
        score_bias = sb("score_bias", [P, HEADS, T])
        own = sb("own", [P, NB])
        part_i = sb("part_i", [128, 1], i32)
        part = sb("part", [128, 1])
        strip_i = sb("strip_i", [128, 1], i32)
        strip = sb("strip", [128, 1])
        heads_i = sb("heads_i", [128, HB], i32)
        in_head = sb("in_head", [128, HB])
        bq_q = sb("bq_q", [128, KC])
        bk_head = sb("bk_head", [128, KC, HB])
        experts_i = sb("experts_i", [128, E], i32)
        experts = sb("experts", [128, E])
        region = sb("region", [128, E])
        steps_i = sb("steps_i", [128, MAXT], i32)
        steps = sb("steps", [128, MAXT])
        live = sb("live", [128, 1])
        spill = sb("spill", [128, K])
        pad_rows = sb("pad_rows", [128, 2, ROW])
        eps = sb("eps", [P, 1])
        minus_half = sb("minus_half", [P, 1])

        x_sb = sb("x_sb", [N_IN, 2, NB * D])
        h_sb = sb("h_sb", [P, 2, D])
        hbo = sb("hbo", [P, 2, D])
        stats = sb("stats", [P, 6])
        mv = sb("mv", [P, 2])
        var_eps = sb("var_eps", [P, 1])
        rstd = sb("rstd", [P, 1])
        xn = sb("xn", [P, D])
        xTs = sb("xTs", [128, 2 * KC, P])
        xT, x2T = xTs[:, 0:KC, :], xTs[:, KC:2 * KC, :]
        qT = sb("qT", [128, 2, KC, NB * (P + T)])
        kT = sb("kT", [128, 2, KC, HB, P])
        va = sb("va", [P, 2, HPAIRS, 3, HD])
        sc = sb("sc", [P, KC, HB, T])
        mx = sb("mx", [P, KC, HB])
        sm = sb("sm", [P, KC, HB, T])
        ex = sb("ex", [P, KC, HB, T])
        pr = sb("pr", [P, KC, HB, NB, T])
        pr_sum = sb("pr_sum", [P, KC, HB])
        rsum = sb("rsum", [P, KC, HB])
        weight = sb("weight", [P, KC, HB, NB])
        prT = sb("prT", [P, HEADS, P])
        cxT = sb("cxT", [128, KC, P])
        h2 = sb("h2", [P, 2, D])
        stats2 = sb("stats2", [P, 6])
        mv2 = sb("mv2", [P, 2])
        var_eps2 = sb("var_eps2", [P, 1])
        rstd2 = sb("rstd2", [P, 1])
        rows = sb("rows", [P, 2, K, ROW])
        lg = sb("lg", [P, E])
        top = sb("top", [P, 8])
        top_i = sb("top_i", [P, 8], u32)
        neg_top = sb("neg_top", [P, 1])
        choice = sb("choice", [P, K])
        hot = sb("hot", [P, K, E])
        hot_any = sb("hot_any", [P, E])
        gexp = sb("gexp", [P, K])
        gsum = sb("gsum", [P, 1])
        grec = sb("grec", [P, 1])
        gate = sb("gate", [P, K])
        count = sb("count", [128, E])
        pos_all = sb("pos_all", [P, E])
        pos_hot = sb("pos_hot", [P, K, E])
        pos = sb("pos", [P, K])
        keep = sb("keep", [P, K])
        dest_f = sb("dest_f", [P, K])
        dest = sb("dest", [P, 2, K], i32)
        token = sb("token", [128, 1])

        full = sb("full", [128, E, MAXT])
        ntiles = sb("ntiles", [128, E])
        first = sb("first", [128, E + 1])
        origin = sb("origin", [128, E])
        first_i = sb("first_i", [128, E + 1], i32)
        origin_i = sb("origin_i", [128, E], i32)
        pad_row = sb("pad_row", [128, E])
        pad_row_i = sb("pad_row_i", [128, E], i32)

        st1 = sb("st1", [128, KC, HID])
        st2 = sb("st2", [128, HC, D])
        w1h = sb("w1h", [128, 2, KC, HID], f32r)
        w1l = sb("w1l", [128, 2, KC, HID], f32r)
        w2h = sb("w2h", [128, 2, HC, D], f32r)
        w2l = sb("w2l", [128, 2, HC, D], f32r)
        xr = sb("xr", [128, 2, ROW])
        meta_next = sb("meta_next", [128, 2, 2])
        meta = sb("meta", [128, 2, 2])
        xh = sb("xh", [128, KC, TILE], f32r)
        xl = sb("xl", [128, KC, TILE], f32r)
        hf = kT[:, :, :, :, :].rearrange("p r c h k -> p (r c h k)")[:, 0:HC * TILE].rearrange("p (j n) -> p j n", j=HC)
        hh = sb("hh", [128, HC, TILE], f32r)
        hl = sb("hl", [128, HC, TILE], f32r)
        b1_cur = sb("b1_cur", [128, HC])
        b2_cur = sb("b2_cur", [128, D])
        yb = sb("yb", [128, 2, D])
        y = sb("y", [128, 2, D])
        y_dest = sb("y_dest", [128, 2], i32)

        banks = [ctx.enter_context(nc.psum_tensor(f"bank{i}", [128, 512], fp32)) for i in range(8)]
        ps_scores, ps_probT = banks[0:2], banks[2:4]
        ps_ctx, ps_kq, ps_xv, ps_h = banks[4:8]
        LG = slice(HB * T, HB * T + E)
        RANK, COUNT = LG, slice(HB * T + E, HB * T + 2 * E)
        ps_hidden, ps_y, ps_xT = banks[0:4], banks[4:6], banks[6]

        const_loaded, proj_loaded, b2_loaded = sem("const_loaded"), sem("proj_loaded"), sem("b2_loaded")
        x_loaded, x_filled = [sem("x_loaded0"), sem("x_loaded1")], sem("x_filled")
        stage0_loaded, stage_loaded = sem("stage0_loaded"), sem("stage_loaded")
        iotas_made, masks_made, pool_order = sem("iotas_made"), sem("masks_made"), sem("pool_order")
        dve_order = sem("dve_order")
        levels_made, wave_mm, wave_made = sem("levels_made"), sem("wave_mm"), sem("wave_made")
        vec_mm, setup_done = sem("vec_mm"), sem("setup_done")
        h_mm, h_done, hbo_done = sem("h_mm"), sem("h_done"), sem("hbo_done")
        mv_done, rstd_done = sem("mv_done"), sem("rstd_done")
        xn_done, xTs_mm, xTs_done = sem("xn_done"), sem("xTs_mm"), sem("xTs_done")
        kq_mm, kv_mm = sem("kq_mm"), sem("kv_mm")
        q_done, k0_done, k1_done, v_done = sem("q_done"), sem("k0_done"), sem("k1_done"), sem("v_done")
        s_mm, sc_done, mx_done, sm_done = sem("s_mm"), sem("sc_done"), sem("mx_done"), sem("sm_done")
        psum_done, rsum_done, weight_done = sem("psum_done"), sem("rsum_done"), sem("weight_done")
        exp_done, pr0_done, pr1_done = sem("exp_done"), sem("pr0_done"), sem("pr1_done")
        prT_mm, prT_done = sem("prT_mm"), sem("prT_done")
        cxT_mm, cxT_done, wo_mm, h2_done = sem("cxT_mm"), sem("cxT_done"), sem("wo_mm"), sem("h2_done")
        mv2_done, rstd2_done = sem("mv2_done"), sem("rstd2_done")
        h2_stored = [sem("h2_stored0"), sem("h2_stored1")]
        row0_done, row1_done = sem("row0_done"), sem("row1_done")
        lg_mm, top_done, hot_done, rank_mm = sem("lg_mm"), sem("top_done"), sem("hot_done"), sem("rank_mm")
        gexp_done, rank_read, dest_done = sem("gexp_done"), sem("rank_read"), sem("dest_done")
        scattered = [sem("scattered0"), sem("scattered1")]
        tables_done, pads_written = sem("tables_done"), sem("pads_written")
        high_done, low_done = sem("high_done"), sem("low_done")
        xr_loaded, xr_mm, meta_taken, xh_done, xs_done = (
            sem("xr_loaded"), sem("xr_mm"), sem("meta_taken"), sem("xh_done"), sem("xs_done"))
        hid_mm, hf_done, hs_done, y_mm, y_read, y_ready, y_added = (
            sem("hid_mm"), sem("hf_done"), sem("hs_done"), sem("y_mm"), sem("y_read"), sem("y_ready"), sem("y_added"))
        y_free, meta_kept, hh_done = sem("y_free"), sem("meta_kept"), sem("hh_done")
        ONE = 1
        act_b1 = sem("act_b1")

        def head(q, i):
            return 8 * (i // 2) + 2 * q + i % 2

        def num(g):
            return 2 * g[0] + g[1]

        def by(g, k):
            return (g[0] + (g[1] + k) // 2, (g[1] + k) % 2)

        def exists(g):
            return not isinstance(g[0], int) or 0 <= num(g) < GROUPS

        def over_groups(eng, step):
            for i in (0, 1):
                for r in (0, 1):
                    step((i, r))
            with eng.Fori(2, PAIRS - 1) as pair:
                for r in (0, 1):
                    step((pair, r))
            for i in (PAIRS - 1, PAIRS):
                for r in (0, 1):
                    step((i, r))

        def is_last(g):
            return isinstance(g[0], int) and num(g) == GROUPS - 1

        def up_to(value, most):
            return min(value, most) if isinstance(value, int) else value

        def load_table(eng, table, index):
            return eng.value_load(table[0:1, ds(index, 1)] if not isinstance(index, int)
                                  else table[0:1, index:index + 1], min_val=0, max_val=E * REGION)

        CHUNKS = 4

        def chunk(slot, i):
            if i < 2:
                return st1[:, i, :], w1h[:, slot, i, :], w1l[:, slot, i, :]
            j = slice((i - 2) * HC // 2, (i - 1) * HC // 2)
            return st2[:, j, :], w2h[:, slot, j, :], w2l[:, slot, j, :]

        def normal(eng, c):
            return eng.tensor_tensor(pr[:, c, :, :, :], ex[:, c, :, :].unsqueeze(2).broadcast_to([P, HB, NB, T]),
                                     weight[:, c, :, :].unsqueeze(3).broadcast_to([P, HB, NB, T]), ALU.mult)

        block = ctx.enter_context(nc.Block())

        @block.sync
        def _(sp):
            sp.dma_start(h0_bc[:, :], h0.partition_broadcast(128)).then_inc(const_loaded, 16)
            x_v = x.rearrange("b n d -> n b d")

            def load_x(g):
                dst = x_sb[:, g[1], :].rearrange("n (b d) -> n b d", b=NB)
                if is_last(g):
                    sp.dma_start(dst[:, LAST_BATCHES:NB, :], x_v[:, 0:NB - LAST_BATCHES, :]).then_inc(x_filled, 16)
                    sp.wait_ge(x_filled, 16)
                    sp.dma_start(dst[:, 0:LAST_BATCHES, :], x_v[:, B - LAST_BATCHES:B, :]).then_inc(x_loaded[g[1]], 16)
                else:
                    sp.dma_start(dst, x_v[:, ds(NB * num(g), NB), :]).then_inc(x_loaded[g[1]], 16)

            load_x((0, 0))
            sp.dma_start(wq_sb[:, :, :], wq.rearrange("(c p) n -> p c n", p=128)).then_inc(proj_loaded, 16)
            sp.dma_start(wk_sb[:, :, :], wk.rearrange("(c p) n -> p c n", p=128)).then_inc(proj_loaded, 16)
            sp.dma_start(wv_sb[:, :, :], wv.rearrange("(c p) n -> p c n", p=128)).then_inc(proj_loaded, 16)
            load_x((0, 1))
            sp.dma_start(wo_sb[:, :, :], wo.rearrange("(c p) n -> p c n", p=128)).then_inc(proj_loaded, 16)
            sp.dma_start(wr_sb[:, :, :], w_router.rearrange("(c p) n -> p c n", p=128)).then_inc(proj_loaded, 16)
            sp.dma_start(st1[:, :, :], w1[0, :, :].rearrange("(c p) n -> p c n", p=128)).then_inc(stage0_loaded, 16)
            sp.dma_start(st2[:, :, :], w2[0, :, :].rearrange("(c p) n -> p c n", p=128)).then_inc(stage0_loaded, 16)
            sp.dma_start(b2_bc[:, :, :].rearrange("p e d -> p (e d)"),
                         b2.rearrange("e d -> (e d)").partition_broadcast(128)).then_inc(b2_loaded, 16)

            def store_h2(g):
                sp.wait_ge(h2_done, num(g) + 1)
                sp.dma_start(out[ds(P * num(g), P), :], h2[:, g[1], :]).then_inc(h2_stored[g[1]], 16)

            def step(g):
                if exists(by(g, 2)):
                    sp.wait_ge(h_mm, num(g) + 1)
                    load_x(by(g, 2))
                if exists(by(g, -3)):
                    store_h2(by(g, -3))

            for i in (0, 1):
                for r in (0, 1):
                    step((i, r))
            with sp.Fori(2, PAIRS - 2) as pair:
                for r in (0, 1):
                    step((pair, r))
            for i in range(PAIRS - 2, PAIRS + 2):
                for r in (0, 1):
                    step((i, r))

            sp.wait_ge(tables_done, 1)
            for e in range(E):
                row = nc.s_assert_within(
                    load_table(sp, pad_row_i, e), 0, SPILL - TILE,
                    skip_runtime_bounds_check_because="a region holds every token and a tile of padding")
                sp.dma_start(dispatch[ds(row, TILE), :].rearrange("(h p) c -> p h c", h=2), pad_rows[:, :, :])\
                    .then_inc(pads_written, 16)
            for r in (0, 1):
                sp.wait_ge(scattered[r], 16 * K * PAIRS)
            sp.wait_ge(pads_written, 16 * E)
            with sp.Fori(0, E) as e:
                origin_e = load_table(sp, origin_i, e)
                first_e = load_table(sp, first_i, e)
                last_e = load_table(sp, first_i, e + 1)
                with sp.Fori(first_e, last_e) as t:
                    sp.wait_ge(xr_mm, ONE + t)
                    sp.wait_ge(meta_taken, ONE + t)
                    row = nc.s_assert_within(
                        origin_e + TILE * t, 0, SPILL - TILE,
                        skip_runtime_bounds_check_because="a region holds every token and a tile of padding")
                    sp.dma_start(xr[:, :, :], dispatch[ds(row, TILE), :].rearrange("(h p) c -> p h c", h=2))\
                        .then_inc(xr_loaded, 16)
            total = load_table(sp, first_i, E)
            sp.wait_ge(xr_mm, ONE + total)
            sp.wait_ge(meta_taken, ONE + total)
            sp.dma_start(xr[:, :, :], dispatch[0:TILE, :].rearrange("(h p) c -> p h c", h=2)).then_inc(xr_loaded, 16)
            sp.wait_ge(y_added, 32 * total)
            stand(sp)

        @block.gpsimd
        def _(pool):
            pool.iota(tap1_i[:, :], pattern=[[1, N_IN]], base=PAD1, channel_multiplier=-2)
            pool.iota(tap2_i[:, :], pattern=[[-2, T]], base=PAD2, channel_multiplier=1).then_inc(iotas_made, 1)
            pool.memset(ident[:, :], 0.0).then_inc(pool_order, 1)
            pool.memset(wave[:, :, :], 0.0).then_inc(masks_made, 1)
            pool.wait_ge(pool_order, 1)
            pool.affine_select(out=ident[:, :], in_=ident[:, :], compare_op=ALU.not_equal, fill=1.0, base=0,
                               pattern=[[-1, 128]], channel_multiplier=1).then_inc(masks_made, 1)
            pool.iota(rel_i[:, :], pattern=[[1, T]], base=0, channel_multiplier=-1)
            pool.iota(heads_i[:, :], pattern=[[1, HB]], base=0, channel_multiplier=0)
            pool.iota(part_i[:, :], pattern=[[0, 1]], base=0, channel_multiplier=1)
            pool.iota(experts_i[:, :], pattern=[[1, E]], base=0, channel_multiplier=0)
            pool.iota(steps_i[:, :], pattern=[[TILE, MAXT]], base=0, channel_multiplier=0).then_inc(iotas_made, 1)
            pool.memset(before[:, :], 1.0).then_inc(pool_order, 1)
            pool.memset(ones[:, :], 1.0)
            pool.memset(qT[:, :, :, :], 0.0)
            pool.memset(eps[:, :], EPS)
            pool.memset(minus_half[:, :], -0.5)
            pool.memset(va[:, :, :, :, :].rearrange("p a h z v -> p (a h z v)"), 0.0)
            pool.memset(pad_rows[:, :, :], 0.0).then_inc(masks_made, 1)
            pool.wait_ge(pool_order, 2)
            pool.affine_select(out=before[:, :], in_=before[:, :], compare_op=ALU.is_gt, fill=0.0, base=0,
                               pattern=[[1, P]], channel_multiplier=-1).then_inc(masks_made, 1)
            def bias_rows(g):
                n = num(g)
                pool.wait_ge(h_done, n + 1)
                wait(pool, h2_done, n - 1)
                pool.tensor_tensor(hbo[:, g[1], :], h_sb[:, g[1], :], bo_bc[:, :], ALU.add).then_inc(hbo_done, 1)

            def root(g, of, m, v, r, var_ready, ready):
                pool.wait_ge(var_ready, num(g) + 1)
                pool.tensor_tensor(v[:, :], m[:, 1:2], eps[:, :], ALU.add).then_inc(of, 1)
                pool.wait_ge(of, num(g) + 1)
                pool.tensor_tensor(r[:, :], v[:, :], minus_half[:, :], ALU.pow).then_inc(ready, 1)

            var1, var2 = sem("var1"), sem("var2")

            def root1(g):
                root(g, var1, mv, var_eps, rstd, mv_done, rstd_done)

            def root2(g):
                root(g, var2, mv2, var_eps2, rstd2, mv2_done, rstd2_done)

            root1((0, 0))
            pool.wait_ge(const_loaded, 16 * 6)
            bias_rows((0, 0))
            root1((0, 1))

            def low_part(e, slot):
                for i in range(CHUNKS):
                    pool.wait_ge(high_done, CHUNKS * e + i + 1)
                    w, high, low = chunk(slot, i)
                    pool.tensor_tensor(low, w, high.bitcast(fp32), ALU.subtract).then_inc(low_done, 1)

            def stage(e):
                pool.wait_ge(low_done, CHUNKS * e)
                stand(pool)
                pool.dma_start(st1[:, :, :], w1[ds(e, 1), :, :].rearrange("e (c p) n -> p (e c) n", p=128))\
                    .then_inc(stage_loaded, 16)
                pool.dma_start(st2[:, :, :], w2[ds(e, 1), :, :].rearrange("e (c p) n -> p (e c) n", p=128))\
                    .then_inc(stage_loaded, 16)

            def normalise(g):
                n = num(g)
                pool.wait_ge(weight_done, KC * n + 1)
                wait(pool, prT_mm, QUADS * n - QUADS + QUADS // KC)
                normal(pool, 0).then_inc(pr0_done, 1)

            def scatter(g):
                pool.wait_ge(dest_done, num(g) + 1)
                pool.wait_ge(row1_done, num(g) + 1)
                stand(pool)
                for k in range(K):
                    pool.indirect_dma_start(dispatch, bass.IndirectOffsetOnAxis(ap=dest[:, g[1], k:k + 1], axis=0),
                                            rows[:, g[1], k, :], None).then_inc(scattered[g[1]], 16)

            def step(g):
                if exists(by(g, 2)):
                    root1(by(g, 2))
                if exists(g):
                    normalise(g)
                if exists(by(g, 1)):
                    bias_rows(by(g, 1))
                if exists(by(g, -1)):
                    root2(by(g, -1))
                if exists(by(g, -2)):
                    scatter(by(g, -2))

            over_groups(pool, step)

            low_part(0, 0)
            stage(1)
            pool.sem_inc(y_free, 2)
            for r in (0, 1):
                pool.wait_ge(h2_stored[r], 16 * PAIRS)

            def tiles(e):
                first_e = load_table(pool, first_i, e)
                last_e = load_table(pool, first_i, e + 1)
                with pool.Fori(first_e, last_e) as t:
                    for half in (0, 1):
                        pool.wait_ge(y_ready, ONE + 2 * t + half + 1)
                        stand(pool)
                        pool.indirect_dma_start(out, bass.IndirectOffsetOnAxis(ap=y_dest[:, half:half + 1], axis=0),
                                                y[:, half, :], None, compute_op=ALU.add).then_inc(y_added, 16)
                        pool.wait_ge(y_added, 32 * t + 16 * half + 16)
                        pool.sem_inc(y_free, 1)

            with pool.Fori(0, E // 2 - 1) as pair:
                for r in (0, 1):
                    e = 2 * pair + r
                    low_part(e + 1, 1 - r)
                    stage(e + 2)
                    tiles(e)
            low_part(E - 1, 1)
            tiles(E - 2)
            tiles(E - 1)

        @block.scalar
        def _(act):
            act.dma_start(vec_rows[0:E * HC, :], b1.rearrange("e (j p) -> (e j) p", p=128)).then_inc(const_loaded, 16)
            act.dma_start(vec_rows[E * HC:E * HC + KC, :], bq.rearrange("(c p) -> c p", p=128)).then_inc(const_loaded, 16)
            act.dma_start(vec_rows[E * HC + KC:E * HC + 2 * KC, :], bk.rearrange("(c p) -> c p", p=128))\
                .then_inc(const_loaded, 16)
            act.dma_start(bv_bc[:, :], bv.partition_broadcast(P)).then_inc(const_loaded, 16)
            act.dma_start(bo_bc[:, :], bo.partition_broadcast(P)).then_inc(const_loaded, 16)

            def h_out(g):
                n = num(g)
                act.wait_ge(h_mm, n + 1)
                wait(act, hbo_done, n - 1)
                wait(act, xn_done, n - 1)
                act.activation(h_sb[:, g[1], :], ps_h[0:P, 0:D], ACT.Copy).then_inc(h_done, 1)

            def xTs_out(a, b):
                act.wait_ge(xTs_mm, num(a) + 1)
                cols = slice(0 if exists(a) else KC, 2 * KC if exists(b) else KC)
                act.activation(xTs[:, cols, :].rearrange("p c n -> p (c n)"), ps_xv[:, cols.start * P:cols.stop * P],
                               ACT.Copy).then_inc(xTs_done, 1)

            def exp(g, c):
                n = KC * num(g) + c
                act.wait_ge(sm_done, n + 1)
                wait(act, (pr0_done, pr1_done)[c], num(g))
                act.activation(ex[:, c, :, :], sm[:, c, :, :], ACT.Exp).then_inc(exp_done, 1)

            def queries_out(g):
                act.wait_ge(kq_mm, num(g) + 1)
                for c in range(KC):
                    last = act.activation(qT[:, g[1], c, :].rearrange("p (b s) -> p b s", b=NB)[:, :, 0:T],
                                          ps_kq[:, (1 + c) * P:(2 + c) * P].rearrange("p (b t) -> p b t", b=NB),
                                          ACT.Identity, bias=bq_q[:, c:c + 1], scale=float(HD) ** -0.5)
                last.then_inc(q_done, 1)

            def keys1_out(g, heads):
                for h in heads:
                    last = act.activation(kT[:, g[1], 1, h, :], ps_kq[:, 0:P], ACT.Identity,
                                          bias=bk_head[:, 1, h:h + 1], scale=in_head[:, h:h + 1])
                if h == HB - 1:
                    last.then_inc(k1_done, 1)

            def second_row(g):
                act.wait_ge(row0_done, num(g) + 1)
                act.activation(rows[:, g[1], 1, 0:D], rows[:, g[1], 0, 0:D], ACT.Copy).then_inc(row1_done, 1)

            def probT_out(g, q):
                n = QUADS * num(g) + q
                act.wait_ge(prT_mm, n + 1)
                wait(act, cxT_mm, num(g))
                act.activation(prT[:, q * QH:(q + 1) * QH, :].rearrange("p h k -> p (h k)"),
                               ps_probT[q % 2][0:P, 0:QH * P], ACT.Copy).then_inc(prT_done, 1)

            def ctxT_out(g):
                act.wait_ge(cxT_mm, num(g) + 1)
                act.activation(cxT[:, :, :].rearrange("p c n -> p (c n)"), ps_ctx[:, 0:KC * P], ACT.Copy)\
                    .then_inc(cxT_done, 1)

            def gate_exp(g):
                act.wait_ge(top_done, num(g) + 1)
                act.activation(gexp[:, :], top[:, 0:K], ACT.Exp, bias=neg_top[:, 0:1],
                               accum_out=gsum[:, 0:1]).then_inc(gexp_done, 1)

            h_out((0, 0))
            xTs_out((0, 0), (-2, 1))
            act.wait_ge(setup_done, 1)
            queries_out((0, 0))
            keys1_out((0, 0), range(HB))
            h_out((0, 1))

            def step(g):
                context, routed = exists(by(g, -1)), exists(by(g, -2))
                if context:
                    probT_out(by(g, -1), 0)
                    probT_out(by(g, -1), 1)
                if exists(by(g, 2)):
                    h_out(by(g, 2))
                if exists(by(g, 1)) or routed:
                    xTs_out(by(g, 1), by(g, -2))
                if exists(g):
                    exp(g, 0)
                if context:
                    probT_out(by(g, -1), 2)
                if exists(g):
                    exp(g, 1)
                if context:
                    probT_out(by(g, -1), 3)
                if routed:
                    second_row(by(g, -2))
                if exists(by(g, 1)):
                    queries_out(by(g, 1))
                    keys1_out(by(g, 1), range(HB // 2))
                if context:
                    ctxT_out(by(g, -1))
                if exists(by(g, 1)):
                    keys1_out(by(g, 1), range(HB // 2, HB))
                if routed:
                    gate_exp(by(g, -2))

            over_groups(act, step)

            def high_part(e, slot, i):
                w, high, low = chunk(slot, i)
                act.activation(high, w, ACT.Copy).then_inc(high_done, 1)

            act.wait_ge(stage0_loaded, 32)
            for i in range(CHUNKS):
                high_part(0, 0, i)

            act.wait_ge(tables_done, 1)

            def x_high(n):
                act.wait_ge(xr_mm, ONE + n)
                act.activation(xh[:, :, :].rearrange("p c n -> p (c n)"), ps_xT[:, :], ACT.Copy).then_inc(xh_done, 1)

            act.sem_inc(hf_done, ONE)
            x_high(1)

            def tile(e, t, slot, opens):
                for b in range(4):
                    act.wait_ge(hid_mm, 4 * t + b + 1)
                    for j in (2 * b, 2 * b + 1):
                        last = act.activation(hf[:, j, :], ps_hidden[b][:, (j % 2) * TILE:(j % 2 + 1) * TILE], ACT.Relu,
                                              bias=b1_cur[:, j:j + 1])
                    last.then_inc(hf_done, 1)
                    if opens and b == 0:
                        act.wait_ge(stage_loaded, 32 * (e + 1))
                    if opens and b < 2:
                        high_part(e + 1, 1 - slot, b)
                x_high(t + 2)
                if opens:
                    high_part(e + 1, 1 - slot, 2)
                    high_part(e + 1, 1 - slot, 3)

            def expert(e, slot, more):
                first_e = load_table(act, first_i, e)
                act.wait_ge(hf_done, ONE + 4 * first_e)
                act.activation(b1_cur[:, :], b1_cols[:, ds(HC * e, HC)], ACT.Copy).then_inc(act_b1, 1)
                act.wait_ge(act_b1, e + 1)
                last_e = load_table(act, first_i, e + 1)
                tile(e, first_e, slot, more)
                with act.Fori(first_e + 1, last_e) as t:
                    tile(e, t, slot, False)

            with act.Fori(0, E // 2 - 1) as pair:
                for slot in (0, 1):
                    expert(2 * pair + slot, slot, True)
            expert(E - 2, 0, True)
            expert(E - 1, 1, False)

        @block.vector
        def _(dve):
            done = [0]

            def link(ins):
                done[0] += 1
                ins.then_inc(dve_order, 1)
                dve.wait_ge(dve_order, done[0])

            dve.wait_ge(iotas_made, 1)
            dve.wait_ge(const_loaded, 16 * 6)
            dve.tensor_copy(tap1[:, :], tap1_i[:, :])
            link(dve.tensor_copy(tap2[:, :], tap2_i[:, :]))
            for tap in range(TAPS):
                for src, hit, level in ((tap1, hit1, level1), (tap2, hit2, level2)):
                    dst = level if tap == 0 else hit
                    last = dve.tensor_scalar(dst[:, :], src[:, :], float(tap), h0_bc[0:N_MID, tap:tap + 1],
                                             ALU.is_equal, ALU.mult)
                link(last)
                if tap:
                    dve.tensor_tensor(level1[:, :], level1[:, :], hit1[:, :], ALU.add)
                    link(dve.tensor_tensor(level2[:, :], level2[:, :], hit2[:, :], ALU.add))
            dve.sem_inc(levels_made, 1)
            dve.wait_ge(iotas_made, 2)
            dve.tensor_copy(rel[:, :], rel_i[:, :])
            dve.tensor_copy(part[:, :], part_i[:, :])
            dve.tensor_copy(experts[:, :], experts_i[:, :])
            dve.tensor_copy(steps[:, :], steps_i[:, :])
            link(dve.tensor_scalar(strip_i[:, :], part_i[:, :], HD.bit_length() - 1, None, ALU.logical_shift_right))
            dve.tensor_copy(in_head[:, :], heads_i[:, :])
            for b in range(NB + 1):
                dve.tensor_scalar(reached[:, b:b + 1], part[0:P, :], float(b * T), None, ALU.is_ge)
            link(dve.tensor_copy(strip[:, :], strip_i[:, :]))
            for b in range(1, NB):
                link(dve.scalar_tensor_tensor(rel[:, :], reached[:, b:b + 1].broadcast_to([P, T]), float(T), rel[:, :],
                                              ALU.mult, ALU.add))
            dve.tensor_tensor(own[:, :], reached[:, 0:NB], reached[:, 1:NB + 1], ALU.subtract)
            dve.tensor_scalar(in_head[:, :], in_head[:, :], strip[:, 0:1], None, ALU.is_equal)
            root = (2.0 ** 8) ** (1.0 / HEADS)
            for h in range(HEADS):
                dve.tensor_scalar(score_bias[:, h, :], rel[:, :], 1.0 / root ** (h + 1), None, ALU.mult)
            dve.tensor_scalar(region[:, :], experts[:, :], float(REGION), None, ALU.mult)
            dve.tensor_scalar(live[:, :], part[:, :], float(LAST_BATCHES * T), None, ALU.is_lt)
            for k in range(K):
                dve.tensor_scalar(spill[:, k:k + 1], part[:, :], float(SPILL + HALF * k), None, ALU.add)
            dve.wait_ge(masks_made, 3)
            for half in (0, 1):
                dve.tensor_scalar(pad_rows[:, half, D:D + 1].bitcast(i32), part[:, :], float(PAD_ROW), None, ALU.add)
            dve.tensor_copy(token[:, :], part[:, :])
            link(dve.memset(count[:, :], 0.0))
            dve.wait_ge(wave_mm, 1)
            for b in range(NB):
                last = dve.tensor_copy(wave[:, b, b * T:(b + 1) * T], ps_kq[0:N_IN, 0:T])
            last.then_inc(wave_made, 1)
            dve.wait_ge(vec_mm, 1)
            link(dve.tensor_copy(vec_cols[:, :], ps_ctx[:, 0:E * HC + 2 * KC]))
            dve.tensor_scalar(bq_q[:, :], bq_cols, float(HD) ** -0.5, None, ALU.mult)
            for c in range(KC):
                last = dve.tensor_scalar(bk_head[:, c, :], in_head[:, :], bk_cols[:, c:c + 1], None, ALU.mult)
            link(last)
            dve.sem_inc(setup_done, 1)
            FIRST, LINKS = 4, 12
            links, at = [0, 0], [None]

            def glink(ins):
                if isinstance(at[0][0], int):
                    link(ins)
                else:
                    links[1] += 1
                    ins.then_inc(dve_order, 1)
                    dve.wait_ge(dve_order, links[0] + LINKS * (num(at[0]) - FIRST) + links[1])

            def moments1(g):
                dve.wait_ge(h_done, num(g) + 1)
                glink(dve.bn_stats(stats[:, :], h_sb[:, g[1], :]))
                stand(dve)
                dve.bn_aggr(mv[:, :], stats[:, :]).then_inc(mv_done, 1)

            def norm1(g):
                dve.wait_ge(rstd_done, num(g) + 1)
                wait(dve, xTs_mm, num(g))
                dve.tensor_scalar(xn[:, :], h_sb[:, g[1], :], mv[:, 0:1], rstd[:, 0:1], ALU.subtract, ALU.mult)\
                    .then_inc(xn_done, 1)

            def keys_values_out(g):
                n, r = num(g), g[1]
                dve.wait_ge(kv_mm, n + 1)
                dve.scalar_tensor_tensor(kT[:, r, 0, :, :], ps_xv[:, D:D + P].unsqueeze(1).broadcast_to([128, HB, P]),
                                         bk_cols[:, 0:1], in_head[:, :].unsqueeze(2).broadcast_to([128, HB, P]),
                                         ALU.add, ALU.mult).then_inc(k0_done, 1)
                wait(dve, cxT_mm, n - 1)
                for odd_head in (0, 1):
                    last = dve.tensor_tensor(va[:, r, :, 2 * odd_head, :],
                                             ps_xv[0:P, 0:D].rearrange("p (j o d) -> p j o d", o=2, d=HD)[:, :, odd_head, :],
                                             bv_bc[:, :].rearrange("p (j o d) -> p j o d", o=2, d=HD)[:, :, odd_head, :],
                                             ALU.add)
                last.then_inc(v_done, 1)

            def scores(g, c):
                n = KC * num(g) + c
                dve.wait_ge(s_mm, n + 1)
                dve.tensor_tensor(sc[:, c, :, :], ps_scores[c][0:P, 0:HB * T].rearrange("p (h k) -> p h k", h=HB),
                                  score_bias[:, c * HB:(c + 1) * HB, :], ALU.add).then_inc(sc_done, 1)
                dve.wait_ge(sc_done, n + 1)
                dve.tensor_reduce(mx[:, c, :], sc[:, c, :, :], X, ALU.max).then_inc(mx_done, 1)
                dve.wait_ge(mx_done, n + 1)
                wait(dve, exp_done, n + 1 - KC)
                dve.tensor_tensor(sm[:, c, :, :], sc[:, c, :, :], mx[:, c, :].unsqueeze(2).broadcast_to([P, HB, T]),
                                  ALU.subtract).then_inc(sm_done, 1)

            def weights(g, c):
                n = KC * num(g) + c
                dve.wait_ge(exp_done, n + 1)
                dve.tensor_reduce(pr_sum[:, c, :], ex[:, c, :, :], X, ALU.add).then_inc(psum_done, 1)
                dve.wait_ge(psum_done, n + 1)
                dve.reciprocal(rsum[:, c, :], pr_sum[:, c, :]).then_inc(rsum_done, 1)
                dve.wait_ge(rsum_done, n + 1)
                wait(dve, (pr0_done, pr1_done)[c], num(g))
                dve.tensor_tensor(weight[:, c, :, :], rsum[:, c, :].unsqueeze(2).broadcast_to([P, HB, NB]),
                                  own[:, :].unsqueeze(1).broadcast_to([P, HB, NB]), ALU.mult).then_inc(weight_done, 1)

            def normalise(g):
                n = num(g)
                dve.wait_ge(weight_done, KC * n + 2)
                wait(dve, prT_mm, QUADS * n)
                normal(dve, 1).then_inc(pr1_done, 1)

            def moments2(g):
                n = num(g)
                r = g[1]
                dve.wait_ge(wo_mm, n + 1)
                dve.wait_ge(hbo_done, n + 1)
                wait(dve, h2_stored[r], 16 * g[0])
                dve.tensor_tensor(h2[:, r, :], ps_ctx[0:P, D:2 * D], hbo[:, r, :], ALU.add).then_inc(h2_done, 1)
                dve.wait_ge(h2_done, n + 1)
                glink(dve.bn_stats(stats2[:, :], h2[:, r, :]))
                stand(dve)
                dve.bn_aggr(mv2[:, :], stats2[:, :]).then_inc(mv2_done, 1)

            def norm2(g):
                dve.wait_ge(rstd2_done, num(g) + 1)
                wait(dve, scattered[g[1]], 16 * K * g[0])
                dve.tensor_scalar(rows[:, g[1], 0, 0:D], h2[:, g[1], :], mv2[:, 0:1], rstd2[:, 0:1],
                                  ALU.subtract, ALU.mult).then_inc(row0_done, 1)

            def choose(g):
                n = num(g)
                dve.wait_ge(lg_mm, n + 1)
                glink(dve.tensor_copy(lg[:, :], ps_scores[0][0:P, LG]))
                stand(dve)
                glink(dve.max(top[:, :], lg[:, :]))
                dve.tensor_scalar(neg_top[:, :], top[:, 0:1], -1.0, None, ALU.mult).then_inc(top_done, 1)
                if not (isinstance(g[0], int) and n == 0):
                    dve.tensor_scalar(token[:, :], token[:, :], float(P), None, ALU.add)
                glink(dve.max_index(top_i[:, :], top[:, :], lg[:, :]))
                glink(dve.tensor_copy(choice[:, :], top_i[:, 0:K]))
                glink(dve.tensor_tensor(hot[:, :, :], experts[0:P, :].unsqueeze(1).broadcast_to([P, K, E]),
                                        choice[:, :].unsqueeze(2).broadcast_to([P, K, E]), ALU.is_equal))
                if is_last(g):
                    link_last(dve.tensor_scalar(hot[:, :, :], hot[:, :, :], live[0:P, 0:1], None, ALU.mult))
                dve.tensor_tensor(hot_any[:, :], hot[:, 0, :], hot[:, 1, :], ALU.add).then_inc(hot_done, 1)

            last_links = [0]
            last_order = sem("last_order")

            def link_last(ins):
                last_links[0] += 1
                ins.then_inc(last_order, 1)
                dve.wait_ge(last_order, last_links[0])

            def place(g):
                n = num(g)
                r = g[1]
                dve.wait_ge(rank_mm, n + 1)
                glink(dve.tensor_tensor(pos_all[:, :], ps_scores[1][0:P, RANK], count[0:P, :], ALU.add))
                dve.tensor_tensor(count[:, :], ps_scores[1][:, COUNT], count[:, :], ALU.add).then_inc(rank_read, 1)
                glink(dve.tensor_tensor(pos_hot[:, :, :], hot[:, :, :], pos_all[:, :].unsqueeze(1).broadcast_to([P, K, E]),
                                        ALU.mult))
                glink(dve.tensor_reduce(pos[:, :], pos_hot[:, :, :], X, ALU.add))
                dve.wait_ge(gexp_done, n + 1)
                dve.reciprocal(grec[:, :], gsum[:, :])
                dve.tensor_scalar(keep[:, :], pos[:, :], float(CAP), None, ALU.is_lt)
                glink(dve.scalar_tensor_tensor(dest_f[:, :], choice[:, :], float(REGION), pos[:, :], ALU.mult, ALU.add))
                if is_last(g):
                    link_last(dve.tensor_scalar(dest_f[:, :], dest_f[:, :], live[0:P, 0:1], None, ALU.mult))
                    link_last(dve.tensor_scalar(keep[:, :], keep[:, :], live[0:P, 0:1], None, ALU.mult))
                    dve.tensor_scalar(neg_top[:, :], live[0:P, :], -1.0, 1.0, ALU.mult, ALU.add)
                    link_last(dve.tensor_scalar(gate[:, :], spill[0:P, :], 1.0, None, ALU.mult))
                    link_last(dve.tensor_scalar(gate[:, :], gate[:, :], neg_top[:, 0:1], None, ALU.mult))
                    link_last(dve.tensor_tensor(dest_f[:, :], dest_f[:, :], gate[:, :], ALU.add))
                dve.tensor_copy(dest[:, r, :], dest_f[:, :])
                glink(dve.tensor_scalar(gate[:, :], gexp[:, :], grec[:, 0:1], None, ALU.mult))
                dve.tensor_tensor(rows[:, r, :, D + 1], gate[:, :], keep[:, :], ALU.mult)
                for k in range(K):
                    last = dve.tensor_copy(rows[:, r, k, D:D + 1].bitcast(i32), token[0:P, :])
                last.then_inc(dest_done, 1)

            at[0] = (0, 0)
            moments1((0, 0))
            norm1((0, 0))
            keys_values_out((0, 0))
            moments1((0, 1))
            norm1((0, 1))

            def step(g):
                if isinstance(at[0][0], int):
                    links[0] = done[0]
                at[0], links[1] = g, 0
                if exists(by(g, 2)):
                    moments1(by(g, 2))
                if exists(g):
                    scores(g, 0)
                    scores(g, 1)
                    weights(g, 0)
                    weights(g, 1)
                    normalise(g)
                if exists(by(g, -2)):
                    choose(by(g, -2))
                if exists(by(g, 2)):
                    norm1(by(g, 2))
                if exists(by(g, 1)):
                    keys_values_out(by(g, 1))
                if exists(by(g, -1)):
                    moments2(by(g, -1))
                if exists(by(g, -2)):
                    place(by(g, -2))
                if exists(by(g, -1)):
                    norm2(by(g, -1))
                if not isinstance(g[0], int):
                    assert links[1] == LINKS
                    done[0] = links[0] + LINKS * (GROUPS - 2 - FIRST)

            over_groups(dve, step)

            dve.wait_ge(rank_read, GROUPS)
            dve.tensor_tensor(pad_row[:, :], count[:, :], region[:, :], ALU.add)
            link(dve.tensor_tensor(full[:, :, :], count[:, :].unsqueeze(2).broadcast_to([128, E, MAXT]),
                                   steps[:, :].unsqueeze(1).broadcast_to([128, E, MAXT]), ALU.is_gt))
            dve.tensor_copy(pad_row_i[:, :], pad_row[:, :])
            link(dve.tensor_reduce(ntiles[:, :], full[:, :, :], X, ALU.add))
            dve.memset(first[:, 0:1], 0.0)
            link(dve.tensor_scalar(ntiles[:, :], ntiles[:, :], 1.0, None, ALU.max))
            for e in range(E):
                link(dve.tensor_tensor(first[:, e + 1:e + 2], first[:, e:e + 1], ntiles[:, e:e + 1], ALU.add))
            dve.tensor_copy(first_i[:, :], first[:, :])
            link(dve.scalar_tensor_tensor(origin[:, :], first[:, 0:E], -float(TILE), region[:, :], ALU.mult, ALU.add))
            link(dve.tensor_copy(origin_i[:, :], origin[:, :]))
            dve.sem_inc(tables_done, 1)

            def x_low(t):
                dve.wait_ge(xr_loaded, 16 * (t + 1))
                wait(dve, meta_kept, t)
                dve.tensor_copy(meta_next[:, :, :], xr[:, :, D:ROW]).then_inc(meta_taken, 1)
                dve.wait_ge(xh_done, t + 1)
                dve.tensor_tensor(xl[:, :, :].rearrange("p c n -> p (c n)"), ps_xT[:, :],
                                  xh[:, :, :].bitcast(fp32).rearrange("p c n -> p (c n)"), ALU.subtract).then_inc(xs_done, 1)

            for s in (meta_taken, y_read, y_ready):
                dve.sem_inc(s, ONE)
            x_low(0)
            dve.wait_ge(b2_loaded, 16)
            with dve.Fori(0, E) as e:
                first_e = load_table(dve, first_i, e)
                dve.wait_ge(y_read, ONE + 2 * first_e)
                dve.tensor_copy(b2_cur[:, :], b2_bc[:, ds(e, 1), :].rearrange("p e d -> p (e d)"))
                last_e = load_table(dve, first_i, e + 1)
                with dve.Fori(first_e, last_e) as t:
                    dve.wait_ge(y_ready, ONE + 2 * t)
                    dve.wait_ge(meta_taken, ONE + t + 1)
                    dve.tensor_copy(meta[:, :, :], meta_next[:, :, :]).then_inc(meta_kept, 1)
                    for b in range(4):
                        dve.wait_ge(hf_done, ONE + 4 * t + b + 1)
                        dve.tensor_copy(hh[:, 2 * b:2 * b + 2, :], hf[:, 2 * b:2 * b + 2, :]).then_inc(hh_done, 1)
                        dve.wait_ge(hh_done, 4 * t + b + 1)
                        dve.tensor_tensor(hl[:, 2 * b:2 * b + 2, :], hf[:, 2 * b:2 * b + 2, :],
                                          hh[:, 2 * b:2 * b + 2, :].bitcast(fp32), ALU.subtract).then_inc(hs_done, 1)
                    x_low(t + 1)
                    for half in (0, 1):
                        n = 2 * t + half
                        dve.wait_ge(y_mm, ONE + n + 1)
                        dve.tensor_tensor(yb[:, half, :], ps_y[half][:, 0:D], b2_cur[:, :], ALU.add).then_inc(y_read, 1)
                        dve.wait_ge(y_free, n + 1)
                        dve.wait_ge(y_read, ONE + n + 1)
                        dve.tensor_copy(y_dest[:, half:half + 1], meta[:, half, 0:1].bitcast(i32))
                        dve.tensor_scalar(y[:, half, :], yb[:, half, :], meta[:, half, 1:2], None, ALU.mult)\
                            .then_inc(y_ready, 1)

        @block.tensor
        def _(pe):
            def transposes(dst, src, rows_, cols):
                for c in range(KC):
                    last = pe.transpose(dst[:, c * cols:(c + 1) * cols], src[:, c * 128:(c + 1) * 128],
                                        ident[0:rows_, 0:rows_])
                return last

            pe.wait_ge(levels_made, 1)
            pe.matmul(ps_kq[0:N_IN, 0:T], level1[:, :], level2[:, :], start=True, stop=True).then_inc(wave_mm, 1)
            pe.wait_ge(masks_made, 4)
            pe.wait_ge(const_loaded, 16 * 6)
            n_vec = E * HC + 2 * KC
            pe.transpose(ps_ctx[:, 0:n_vec], vec_rows[0:n_vec, :], ident[0:n_vec, 0:n_vec]).then_inc(vec_mm, 1)
            pe.wait_ge(wave_made, 1)

            def wavelet(g):
                r = g[1]
                pe.wait_ge(x_loaded[r], 16 * (g[0] + 1))
                wait(pe, h_done, num(g))
                for b in range(NB):
                    last = pe.matmul(ps_h[0:P, 0:D], wave[:, b, :], x_sb[:, r, b * D:(b + 1) * D],
                                     start=(b == 0), stop=(b == NB - 1))
                last.then_inc(h_mm, 1)

            def norms_T(a, b):
                if exists(a):
                    pe.wait_ge(xn_done, num(a) + 1)
                wait(pe, v_done, up_to(num(a), GROUPS))
                if exists(a):
                    last = transposes(ps_xv, xn, P, P)
                if exists(b):
                    pe.wait_ge(row0_done, num(b) + 1)
                    last = transposes(ps_xv[:, KC * P:2 * KC * P], rows[:, b[1], 0, :], P, P)
                last.then_inc(xTs_mm, 1)

            def qkv(g):
                pe.wait_ge(xTs_done, num(g) + 1)
                wait(pe, k1_done, num(g))

                def projected(dst, w, m):
                    for c in range(KC):
                        last = pe.matmul(dst, w[:, c, m * 128:(m + 1) * 128], xT[:, c, :], start=(c == 0), stop=(c == KC - 1))
                    return last

                projected(ps_kq[:, P:2 * P], wq_sb, 0)
                projected(ps_kq[:, 2 * P:3 * P], wq_sb, 1)
                projected(ps_kq[:, 0:P], wk_sb, 1).then_inc(kq_mm, 1)
                projected(ps_xv[:, D:D + P], wk_sb, 0)
                for c in range(KC):
                    last = pe.matmul(ps_xv[0:P, 0:D], xT[:, c, :], wv_sb[:, c, :], start=(c == 0), stop=(c == KC - 1))
                last.then_inc(kv_mm, 1)

            def scores(g, c):
                n = KC * num(g) + c
                pe.wait_ge(q_done, num(g) + 1)
                pe.wait_ge((k0_done, k1_done)[c], num(g) + 1)
                wait(pe, sc_done, n + 1 - KC)
                wait(pe, (top_done, rank_read)[c], num(g) - 2)
                for b in range(NB):
                    last = pe.matmul(ps_scores[c][0:P, 0:HB * T], qT[:, g[1], c, b * P:(b + 1) * P],
                                     kT[:, g[1], c, :, b * T:(b + 1) * T], start=(b == 0), stop=(b == NB - 1))
                last.then_inc(s_mm, 1)

            def prob_T(g, q):
                n = QUADS * num(g) + q
                c = q // (QUADS // KC)
                pe.wait_ge((pr0_done, pr1_done)[c], num(g) + 1)
                wait(pe, prT_done, n - 1)
                for i in range(QH):
                    last = pe.transpose(ps_probT[q % 2][0:P, i * P:(i + 1) * P],
                                        pr[:, c, (q * QH + i) % HB, :, :].rearrange("p b k -> p (b k)"),
                                        ident[0:P, 0:P])
                last.then_inc(prT_mm, 1)

            def values(g):
                pe.wait_ge(prT_done, QUADS * num(g) + QUADS)
                pe.wait_ge(v_done, num(g) + 1)
                wait(pe, cxT_done, num(g))
                wait(pe, h2_done, num(g))
                for c in range(KC):
                    for odd_head in (0, 1):
                        for j in range(HPAIRS // KC):
                            pair_ = HPAIRS // KC * c + j
                            last = pe.matmul(ps_ctx[32 * j:32 * j + 32, c * P:(c + 1) * P],
                                             va[:, g[1], pair_, odd_head:odd_head + 2, :].rearrange("p z d -> p (z d)"),
                                             prT[:, 2 * pair_ + odd_head, :], start=(odd_head == 0), stop=(odd_head == 1))
                last.then_inc(cxT_mm, 1)

            def project(g):
                pe.wait_ge(cxT_done, num(g) + 1)
                for c in range(KC):
                    last = pe.matmul(ps_ctx[0:P, D:2 * D], cxT[:, c, :], wo_sb[:, c, :], start=(c == 0), stop=(c == KC - 1))
                last.then_inc(wo_mm, 1)

            def route(g):
                pe.wait_ge(xTs_done, num(g) + 4)
                pe.wait_ge(sc_done, up_to(KC * (num(g) + 2) + 1, KC * GROUPS))
                for c in range(KC):
                    last = pe.matmul(ps_scores[0][0:P, LG], x2T[:, c, :], wr_sb[:, c, :], start=(c == 0), stop=(c == KC - 1))
                last.then_inc(lg_mm, 1)

            def rank(g):
                pe.wait_ge(hot_done, num(g) + 1)
                pe.wait_ge(sc_done, up_to(KC * (num(g) + 2) + 2, KC * GROUPS))
                pe.matmul(ps_scores[1][0:P, RANK], before[:, :], hot_any[:, :], start=True, stop=True)
                pe.matmul(ps_scores[1][:, COUNT], ones[:, :], hot_any[:, :], start=True, stop=True).then_inc(rank_mm, 1)

            pe.wait_ge(proj_loaded, 16 * 5)
            wavelet((0, 0))
            norms_T((0, 0), (-2, 1))
            pe.wait_ge(setup_done, 1)
            qkv((0, 0))
            wavelet((0, 1))

            def step(g):
                context, routed = exists(by(g, -1)), exists(by(g, -2))
                if context:
                    prob_T(by(g, -1), 0)
                    prob_T(by(g, -1), 1)
                if exists(by(g, 2)):
                    wavelet(by(g, 2))
                if exists(g):
                    scores(g, 0)
                if exists(by(g, 1)) or routed:
                    norms_T(by(g, 1), by(g, -2))
                if exists(g):
                    scores(g, 1)
                if context:
                    prob_T(by(g, -1), 2)
                    prob_T(by(g, -1), 3)
                if routed:
                    route(by(g, -2))
                if exists(by(g, 1)):
                    qkv(by(g, 1))
                if context:
                    values(by(g, -1))
                if context:
                    project(by(g, -1))
                if routed:
                    rank(by(g, -2))

            over_groups(pe, step)

            pe.wait_ge(tables_done, 1)

            def row_T(n):
                pe.wait_ge(xr_loaded, 16 * n)
                for c in range(KC):
                    for half in (0, 1):
                        last = pe.transpose(ps_xT[:, c * TILE + half * HALF:c * TILE + (half + 1) * HALF],
                                            xr[:, half, c * 128:(c + 1) * 128], ident[:, :])
                last.then_inc(xr_mm, 1)

            for s in (xr_mm, y_mm):
                pe.sem_inc(s, ONE)
            row_T(1)
            with pe.Fori(0, E // 2) as pair:
                for slot in (0, 1):
                    e = 2 * pair + slot
                    pe.wait_ge(low_done, CHUNKS * (e + 1))
                    stand(pe)
                    first_e = load_table(pe, first_i, e)
                    last_e = load_table(pe, first_i, e + 1)
                    with pe.Fori(first_e, last_e) as t:
                        pe.wait_ge(xs_done, t + 1)
                        for b in range(4):
                            for j in (2 * b, 2 * b + 1):
                                js = slice(j * 128, (j + 1) * 128)
                                terms = [(w, v, c) for c in range(KC)
                                         for w, v in ((w1h, xh), (w1h, xl), (w1l, xh))]
                                for i, (w, v, c) in enumerate(terms):
                                    last = pe.matmul(ps_hidden[b][:, (j % 2) * TILE:(j % 2 + 1) * TILE], w[:, slot, c, js],
                                                     v[:, c, :], start=(i == 0), stop=(i == len(terms) - 1))
                            last.then_inc(hid_mm, 1)
                        row_T(t + 2)
                        for half in (0, 1):
                            hs = slice(half * HALF, (half + 1) * HALF)
                            pe.wait_ge(y_read, ONE + 2 * t)
                            for j in range(HC):
                                if half == 0 and j % 2 == 0:
                                    pe.wait_ge(hs_done, 4 * t + j // 2 + 1)
                                for i, (v, w) in enumerate(((hh, w2h), (hh, w2l), (hl, w2h))):
                                    last = pe.matmul(ps_y[half][:, 0:D], v[:, j, hs], w[:, slot, j, :],
                                                     start=(j == 0 and i == 0), stop=(j == HC - 1 and i == 2))
                            last.then_inc(y_mm, 1)


_INS = ['x', 'L0_tok_h0', 'L0_attn_Wq', 'L0_attn_bq', 'L0_attn_Wk', 'L0_attn_bk', 'L0_attn_Wv', 'L0_attn_bv',
        'L0_attn_Wo', 'L0_attn_bo', 'L0_ffn_w_router', 'L0_ffn_w1', 'L0_ffn_b1', 'L0_ffn_w2', 'L0_ffn_b2']


def kernel(**inputs):
    import numpy as _np
    import concourse.bacc as _bacc
    from concourse import mybir as _mybir
    from concourse.bass_utils import run_bass_kernel_spmd as _run

    nc = _bacc.Bacc("TRN2", target_bir_lowering=False, num_devices=1)
    arrays, args = {}, []
    for name in _INS:
        a = _np.ascontiguousarray(inputs[name])
        arrays[f"in_{name}"] = a
        args.append(nc.dram_tensor(f"in_{name}", a.shape, _mybir.dt.from_np(a.dtype), kind="ExternalInput").ap())
    args.append(nc.dram_tensor("out_rows", (OUT_ROWS, D), _mybir.dt.float32, kind="ExternalOutput").ap())
    audio_tower(nc, *args)
    r = _run(nc, [arrays], core_ids=[0])
    return _np.asarray(r.results[0]["out_rows"])[0:TOKENS].reshape(B, T, D)
```

```python
import concourse.bass as bass
from concourse import mybir
from contextlib import ExitStack

B, N_IN, D = 64, 125, 256
TAPS = 8
N_MID = (N_IN + TAPS - 1) // 2
T = (N_MID + TAPS - 1) // 2
PAD1 = (2 * (N_MID - 1) - N_IN + TAPS) // 2
PAD2 = (2 * (T - 1) - N_MID + TAPS) // 2
HEADS = 16
HD = D // HEADS
NB = 3
P = NB * T
GROUPS = -(-B // NB)
PAIRS = GROUPS // 2
LAST_BATCHES = B - NB * (GROUPS - 1)
KC = D // 128
HB = HEADS // KC
QH = 4
QUADS = HEADS // QH
HPAIRS = HEADS // 2
E, K, HID = 8, 2, 1024
HC = HID // 128
TOKENS = B * T
CAP = int(1.5 * 4 * 512 * K / E)
HALF = 128
TILE = 2 * HALF
REGION = TOKENS + TILE
ROW = D + 2
SPILL = E * REGION
MAXT = -(-TOKENS // TILE)
PAD_ROW = GROUPS * P
OUT_ROWS = PAD_ROW + TILE
EPS = 1e-5


def audio_tower(nc, x, h0, wq, bq, wk, bk, wv, bv, wo, bo, w_router, w1, b1, w2, b2, out):
    fp32, f32r, i32, u32 = mybir.dt.float32, mybir.dt.float32r, mybir.dt.int32, mybir.dt.uint32
    ALU = mybir.AluOpType
    ACT = mybir.ActivationFunctionType
    X = mybir.AxisListType.X
    ds = bass.ds

    ctx = ExitStack()
    with ctx:
        def sb(name, shape, dt=fp32):
            return ctx.enter_context(nc.sbuf_tensor(name, shape, dt))

        def sem(name):
            return ctx.enter_context(nc.semaphore(name))

        def wait(eng, semaphore, value):
            if not (isinstance(value, int) and value <= 0):
                eng.wait_ge(semaphore, value)

        passed = sem("passed")

        def stand(eng):
            eng.sem_inc(passed, 1)

        dispatch = nc.dram_tensor("dispatch", (SPILL + K * HALF, ROW), fp32).ap()

        h0_bc = sb("h0_bc", [128, TAPS])
        vec_rows = sb("vec_rows", [128, 128])
        vec_cols = sb("vec_cols", [128, E * HC + KC])
        b1_cols = vec_cols[:, 0:E * HC]
        bq_cols = vec_cols[:, E * HC:E * HC + KC]
        bv_bc = sb("bv_bc", [P, D])
        bo_bc = sb("bo_bc", [P, D])
        b2_bc = sb("b2_bc", [128, E, D])
        wq_sb = sb("wq_sb", [128, KC, D])
        wk_sb = sb("wk_sb", [128, KC, D])
        wv_sb = sb("wv_sb", [128, KC, D])
        wo_sb = sb("wo_sb", [128, KC, D])
        wr_sb = sb("wr_sb", [128, KC, E])
        ident = sb("ident", [128, 128])
        before = sb("before", [P, P])
        ones = sb("ones", [P, 128])
        level1 = sb("level1", [N_MID, N_IN])
        level2 = sb("level2", [N_MID, T])
        wave = sb("wave", [N_IN, NB, P])
        rel_i = sb("rel_i", [P, T], i32)
        rel = sb("rel", [P, T])
        reached = sb("reached", [P, NB + 1])
        score_bias = sb("score_bias", [P, HEADS, T])
        own = sb("own", [P, NB])
        part_i = sb("part_i", [128, 1], i32)
        part = sb("part", [128, 1])
        strip_i = sb("strip_i", [128, 1], i32)
        strip = sb("strip", [128, 1])
        heads_i = sb("heads_i", [128, HB], i32)
        in_head = sb("in_head", [128, HB])
        bq_q = sb("bq_q", [128, KC])
        bk_row = sb("bk_row", [1, D])
        experts_i = sb("experts_i", [128, E], i32)
        experts = sb("experts", [128, E])
        region = sb("region", [128, E])
        steps_i = sb("steps_i", [128, 2 * MAXT], i32)
        steps = sb("steps", [128, 2 * MAXT])
        later_i = sb("later_i", [128, E + 1, E], i32)
        later = sb("later", [128, E + 1, E])
        dead = sb("dead", [128, 1])
        live = sb("live", [128, 1])
        spill = sb("spill", [128, K])
        pad_rows = sb("pad_rows", [128, 2, ROW])
        eps = sb("eps", [P, 1])
        minus_half = sb("minus_half", [P, 1])

        x_sb = sb("x_sb", [N_IN, 2, NB * D])
        h_sb = sb("h_sb", [P, 2, D])
        hbo = sb("hbo", [P, 2, D])
        stats = sb("stats", [P, 6])
        mv = sb("mv", [P, 2])
        var_eps = sb("var_eps", [P, 1])
        rstd = sb("rstd", [P, 1])
        xn = sb("xn", [P, D])
        xTs = sb("xTs", [128, 2 * KC, P])
        xT, x2T = xTs[:, 0:KC, :], xTs[:, KC:2 * KC, :]
        qT = sb("qT", [128, 2, KC, NB * (P + T)])
        kT = sb("kT", [128, 2, KC, HB, P])
        keys_mem = kT[:, :, :, :, :].rearrange("p r c h k -> p (r c h k)")
        used = [0]

        def before_keys(n):
            at = used[0]
            used[0] += n * TAPS
            return keys_mem[0:N_MID, at:at + n * TAPS].rearrange("p (n t) -> p n t", t=TAPS)

        tap1_i, tap2_i = before_keys(N_IN).bitcast(i32), before_keys(T).bitcast(i32)
        hit1, hit2 = before_keys(N_IN), before_keys(T)
        va = sb("va", [P, 2, HPAIRS, 3, HD])
        sc = sb("sc", [P, KC, HB, T])
        mx = sb("mx", [P, KC, HB])
        sm = sb("sm", [P, KC, HB, T])
        ex = sb("ex", [P, KC, HB, T])
        pr = sb("pr", [P, KC, HB, NB, T])
        pr_sum = sb("pr_sum", [P, KC, HB])
        rsum = sb("rsum", [P, KC, HB])
        weight = sb("weight", [P, KC, HB, NB])
        prT = sb("prT", [P, HEADS, P])
        cxT = sb("cxT", [128, KC, P])
        h2 = sb("h2", [P, 2, D])
        stats2 = sb("stats2", [P, 6])
        mv2 = sb("mv2", [P, 2])
        var_eps2 = sb("var_eps2", [P, 1])
        rstd2 = sb("rstd2", [P, 1])
        rows = sb("rows", [P, 2, K, ROW])
        lg = sb("lg", [P, E])
        top = sb("top", [P, 8])
        top_i = sb("top_i", [P, 8], u32)
        neg_top = sb("neg_top", [P, 1])
        choice = sb("choice", [P, K])
        hot = sb("hot", [P, K, E])
        hot_any = sb("hot_any", [P, E])
        gexp = sb("gexp", [P, K])
        gsum = sb("gsum", [P, 1])
        grec = sb("grec", [P, 1])
        gate = sb("gate", [P, K])
        count = sb("count", [128, E])
        pos_all = sb("pos_all", [P, E])
        pos_hot = sb("pos_hot", [P, K, E])
        pos = sb("pos", [P, K])
        keep = sb("keep", [P, K])
        dest_f = sb("dest_f", [P, K])
        dest = sb("dest", [P, 2, K], i32)
        token = sb("token", [128, 1])

        full = sb("full", [128, E, 2 * MAXT])
        ntiles = sb("ntiles", [128, E])
        nhalves = sb("nhalves", [128, E])
        before_e = sb("before_e", [128, E + 1, E])
        first = sb("first", [128, E + 1])
        origin = sb("origin", [128, E])
        end = sb("end", [128, E + 1])
        end_i = sb("end_i", [128, E + 1], i32)
        first_i = sb("first_i", [128, E + 1], i32)
        origin_i = sb("origin_i", [128, E], i32)
        pad_row = sb("pad_row", [128, E])
        pad_row_i = sb("pad_row_i", [128, E], i32)

        st1 = sb("st1", [128, KC, HID])
        st2 = sb("st2", [128, HC, D])
        w1h = sb("w1h", [128, 2, KC, HID], f32r)
        w1l = sb("w1l", [128, 2, KC, HID], f32r)
        w2h = sb("w2h", [128, 2, HC, D], f32r)
        w2l = sb("w2l", [128, 2, HC, D], f32r)
        xr = sb("xr", [128, 2, ROW])
        meta_next = sb("meta_next", [128, 2, 2])
        meta = sb("meta", [128, 2, 2])
        xh = sb("xh", [128, KC, TILE], f32r)
        xl = sb("xl", [128, KC, TILE], f32r)
        hf = keys_mem[:, 0:HC * TILE].rearrange("p (j n) -> p j n", j=HC)
        hh = sb("hh", [128, HC, TILE], f32r)
        hl = sb("hl", [128, HC, TILE], f32r)
        b1_cur = sb("b1_cur", [128, HC])
        b2_cur = sb("b2_cur", [128, D])
        yb = sb("yb", [128, 2, D])
        y = sb("y", [128, 2, D])
        y_dest = sb("y_dest", [128, 2], i32)

        banks = [ctx.enter_context(nc.psum_tensor(f"bank{i}", [128, 512], fp32)) for i in range(8)]
        ps_scores, ps_probT = banks[0:2], banks[2:4]
        ps_ctx, ps_kq, ps_xv, ps_h = banks[4:8]
        LG = slice(HB * T, HB * T + E)
        RANK, COUNT = LG, slice(HB * T + E, HB * T + 2 * E)
        ps_hidden, ps_y, ps_xT = banks[0:4], banks[4:6], banks[6]

        taps_loaded, const_loaded, proj_loaded, b2_loaded = sem("taps_loaded"), sem("const_loaded"), sem("proj_loaded"), sem("b2_loaded")
        x_loaded, x_filled = [sem("x_loaded0"), sem("x_loaded1")], sem("x_filled")
        stage0_loaded, stage_loaded = sem("stage0_loaded"), sem("stage_loaded")
        iotas_made, masks_made, pool_order = sem("iotas_made"), sem("masks_made"), sem("pool_order")
        dve_order = sem("dve_order")
        levels_made, wave_mm, wave_made = sem("levels_made"), sem("wave_mm"), sem("wave_made")
        vec_mm, setup_done = sem("vec_mm"), sem("setup_done")
        h_mm, h_done, hbo_done = sem("h_mm"), sem("h_done"), sem("hbo_done")
        mv_done, rstd_done = sem("mv_done"), sem("rstd_done")
        xn_done, xTs_mm, xTs_done = sem("xn_done"), sem("xTs_mm"), sem("xTs_done")
        kq_mm, v_mm = sem("kq_mm"), sem("v_mm")
        q_done, k_done, v_done = sem("q_done"), sem("k_done"), sem("v_done")
        s_mm, sc_done, mx_done, sm_done = sem("s_mm"), sem("sc_done"), sem("mx_done"), sem("sm_done")
        psum_done, rsum_done, weight_done = sem("psum_done"), sem("rsum_done"), sem("weight_done")
        exp_done, pr_done = sem("exp_done"), sem("pr_done")
        prT_mm, prT_done = sem("prT_mm"), sem("prT_done")
        cxT_mm, cxT_done, wo_mm, h2_done = sem("cxT_mm"), sem("cxT_done"), sem("wo_mm"), sem("h2_done")
        mv2_done, rstd2_done = sem("mv2_done"), sem("rstd2_done")
        h2_stored = [sem("h2_stored0"), sem("h2_stored1")]
        row0_done, row1_done = sem("row0_done"), sem("row1_done")
        lg_mm, top_done, hot_done, rank_mm = sem("lg_mm"), sem("top_done"), sem("hot_done"), sem("rank_mm")
        gexp_done, rank_read, dest_done = sem("gexp_done"), sem("rank_read"), sem("dest_done")
        scattered = [sem("scattered0"), sem("scattered1")]
        tables_done, pads_written = sem("tables_done"), [sem("pads_written0"), sem("pads_written1")]
        high_done, low_done = sem("high_done"), sem("low_done")
        xr_loaded, xr_mm, meta_taken, xh_done, xs_done = (
            sem("xr_loaded"), sem("xr_mm"), sem("meta_taken"), sem("xh_done"), sem("xs_done"))
        hid_mm, hf_done, hs_done, y_mm, y_read, y_ready, y_added = (
            sem("hid_mm"), sem("hf_done"), sem("hs_done"), sem("y_mm"), sem("y_read"), sem("y_ready"), sem("y_added"))
        y_free, meta_kept, hh_done = sem("y_free"), sem("meta_kept"), sem("hh_done")
        ONE = 1
        act_b1 = sem("act_b1")

        def num(g):
            return 2 * g[0] + g[1]

        def by(g, k):
            return (g[0] + (g[1] + k) // 2, (g[1] + k) % 2)

        def exists(g):
            return not isinstance(g[0], int) or 0 <= num(g) < GROUPS

        def over_groups(eng, step):
            for i in (0, 1):
                for r in (0, 1):
                    step((i, r))
            with eng.Fori(2, PAIRS - 1) as pair:
                for r in (0, 1):
                    step((pair, r))
            for i in (PAIRS - 1, PAIRS):
                for r in (0, 1):
                    step((i, r))

        def is_last(g):
            return isinstance(g[0], int) and num(g) == GROUPS - 1

        def up_to(value, most):
            return min(value, most) if isinstance(value, int) else value

        def load_table(eng, table, index):
            return eng.value_load(table[0:1, ds(index, 1)] if not isinstance(index, int)
                                  else table[0:1, index:index + 1], min_val=0, max_val=E * REGION)

        CHUNKS = 4

        def chunk(slot, i):
            if i < 2:
                return st1[:, i, :], w1h[:, slot, i, :], w1l[:, slot, i, :]
            j = slice((i - 2) * HC // 2, (i - 1) * HC // 2)
            return st2[:, j, :], w2h[:, slot, j, :], w2l[:, slot, j, :]

        block = ctx.enter_context(nc.Block())

        @block.sync
        def _(sp):
            sp.dma_start(h0_bc[:, :], h0.partition_broadcast(128)).then_inc(taps_loaded, 16)
            x_v = x.rearrange("b n d -> n b d")

            def load_x(g):
                dst = x_sb[:, g[1], :].rearrange("n (b d) -> n b d", b=NB)
                if is_last(g):
                    sp.dma_start(dst[:, LAST_BATCHES:NB, :], x_v[:, 0:NB - LAST_BATCHES, :]).then_inc(x_filled, 16)
                    sp.wait_ge(x_filled, 16)
                    sp.dma_start(dst[:, 0:LAST_BATCHES, :], x_v[:, B - LAST_BATCHES:B, :]).then_inc(x_loaded[g[1]], 16)
                else:
                    sp.dma_start(dst, x_v[:, ds(NB * num(g), NB), :]).then_inc(x_loaded[g[1]], 16)

            load_x((0, 0))
            sp.dma_start(wq_sb[:, :, :], wq.rearrange("(c p) n -> p c n", p=128)).then_inc(proj_loaded, 16)
            sp.dma_start(wk_sb[:, :, :], wk.rearrange("(c p) n -> p c n", p=128)).then_inc(proj_loaded, 16)
            sp.dma_start(wv_sb[:, :, :], wv.rearrange("(c p) n -> p c n", p=128)).then_inc(proj_loaded, 16)
            load_x((0, 1))
            sp.dma_start(wo_sb[:, :, :], wo.rearrange("(c p) n -> p c n", p=128)).then_inc(proj_loaded, 16)
            sp.dma_start(wr_sb[:, :, :], w_router.rearrange("(c p) n -> p c n", p=128)).then_inc(proj_loaded, 16)
            sp.dma_start(st1[:, :, :], w1[0, :, :].rearrange("(c p) n -> p c n", p=128)).then_inc(stage0_loaded, 16)
            sp.dma_start(st2[:, :, :], w2[0, :, :].rearrange("(c p) n -> p c n", p=128)).then_inc(stage0_loaded, 16)
            sp.dma_start(b2_bc[:, :, :].rearrange("p e d -> p (e d)"),
                         b2.rearrange("e d -> (e d)").partition_broadcast(128)).then_inc(b2_loaded, 16)

            def store_h2(g):
                sp.wait_ge(h2_done, num(g) + 1)
                sp.dma_start(out[ds(P * num(g), P), :], h2[:, g[1], :]).then_inc(h2_stored[g[1]], 16)

            def step(g):
                if exists(by(g, 2)):
                    sp.wait_ge(h_mm, num(g) + 1)
                    load_x(by(g, 2))
                if exists(by(g, -3)):
                    store_h2(by(g, -3))

            for i in (0, 1):
                for r in (0, 1):
                    step((i, r))
            with sp.Fori(2, PAIRS - 2) as pair:
                for r in (0, 1):
                    step((pair, r))
            for i in range(PAIRS - 2, PAIRS + 2):
                for r in (0, 1):
                    step((i, r))

            sp.wait_ge(tables_done, 1)

            def pad(e, r):
                row = nc.s_assert_within(
                    load_table(sp, pad_row_i, e), 0, SPILL - TILE,
                    skip_runtime_bounds_check_because="a region holds every token and a tile of padding")
                sp.dma_start(dispatch[ds(row, TILE), :].rearrange("(h p) c -> p h c", h=2), pad_rows[:, :, :])\
                    .then_inc(pads_written[r], 16)

            pad(0, 0)

            def expert_rows(pair, r, more):
                e = 2 * pair + r
                origin_e = load_table(sp, origin_i, e)
                first_e = load_table(sp, first_i, e)
                last_e = load_table(sp, first_i, e + 1)
                sp.wait_ge(pads_written[r], 16 * (pair + 1))
                for i in (0, 1):
                    sp.wait_ge(scattered[i], 16 * K * PAIRS)
                stand(sp)
                with sp.Fori(first_e, last_e) as t:
                    sp.wait_ge(xr_mm, ONE + t)
                    sp.wait_ge(meta_taken, ONE + t)
                    row = nc.s_assert_within(
                        origin_e + TILE * t, 0, SPILL - TILE,
                        skip_runtime_bounds_check_because="a region holds every token and a tile of padding")
                    sp.dma_start(xr[:, :, :], dispatch[ds(row, TILE), :].rearrange("(h p) c -> p h c", h=2))\
                        .then_inc(xr_loaded, 16)
                if more:
                    pad(e + 1, 1 - r)

            with sp.Fori(0, E // 2 - 1) as pair:
                for r in (0, 1):
                    expert_rows(pair, r, True)
            expert_rows(E // 2 - 1, 0, True)
            expert_rows(E // 2 - 1, 1, False)
            total = load_table(sp, first_i, E)
            sp.wait_ge(xr_mm, ONE + total)
            sp.wait_ge(meta_taken, ONE + total)
            sp.dma_start(xr[:, :, :], dispatch[0:TILE, :].rearrange("(h p) c -> p h c", h=2)).then_inc(xr_loaded, 16)
            sp.wait_ge(y_added, 32 * total)
            stand(sp)

        @block.gpsimd
        def _(pool):
            pool.iota(tap1_i[:, :, :], pattern=[[1, N_IN], [-1, TAPS]], base=PAD1, channel_multiplier=-2)
            pool.iota(tap2_i[:, :, :], pattern=[[-2, T], [-1, TAPS]], base=PAD2, channel_multiplier=1).then_inc(iotas_made, 1)
            pool.memset(ident[:, :], 0.0).then_inc(pool_order, 1)
            pool.memset(wave[:, :, :], 0.0).then_inc(masks_made, 1)
            pool.wait_ge(pool_order, 1)
            pool.affine_select(out=ident[:, :], in_=ident[:, :], compare_op=ALU.not_equal, fill=1.0, base=0,
                               pattern=[[-1, 128]], channel_multiplier=1).then_inc(masks_made, 1)
            pool.iota(rel_i[:, :], pattern=[[1, T]], base=0, channel_multiplier=-1)
            pool.iota(heads_i[:, :], pattern=[[1, HB]], base=0, channel_multiplier=0)
            pool.iota(part_i[:, :], pattern=[[0, 1]], base=0, channel_multiplier=1)
            pool.iota(later_i[:, :, :], pattern=[[1, E + 1], [-1, E]], base=0, channel_multiplier=0)
            pool.iota(experts_i[:, :], pattern=[[1, E]], base=0, channel_multiplier=0)
            pool.iota(steps_i[:, :], pattern=[[HALF, 2 * MAXT]], base=0, channel_multiplier=0).then_inc(iotas_made, 1)
            pool.memset(before[:, :], 1.0).then_inc(pool_order, 1)
            pool.memset(ones[:, :], 1.0)
            pool.memset(qT[:, :, :, :], 0.0)
            pool.memset(eps[:, :], EPS)
            pool.memset(minus_half[:, :], -0.5)
            pool.memset(va[:, :, :, :, :].rearrange("p a h z v -> p (a h z v)"), 0.0)
            pool.memset(pad_rows[:, :, :], 0.0).then_inc(masks_made, 1)
            pool.wait_ge(pool_order, 2)
            pool.affine_select(out=before[:, :], in_=before[:, :], compare_op=ALU.is_gt, fill=0.0, base=0,
                               pattern=[[1, P]], channel_multiplier=-1).then_inc(masks_made, 1)

            def bias_rows(g):
                n = num(g)
                pool.wait_ge(h_done, n + 1)
                wait(pool, h2_done, n - 1)
                pool.tensor_tensor(hbo[:, g[1], :], h_sb[:, g[1], :], bo_bc[:, :], ALU.add).then_inc(hbo_done, 1)

            def root(g, of, m, v, r, var_ready, ready):
                pool.wait_ge(var_ready, num(g) + 1)
                pool.tensor_tensor(v[:, :], m[:, 1:2], eps[:, :], ALU.add).then_inc(of, 1)
                pool.wait_ge(of, num(g) + 1)
                pool.tensor_tensor(r[:, :], v[:, :], minus_half[:, :], ALU.pow).then_inc(ready, 1)

            var1, var2 = sem("var1"), sem("var2")

            def root1(g):
                root(g, var1, mv, var_eps, rstd, mv_done, rstd_done)

            def root2(g):
                root(g, var2, mv2, var_eps2, rstd2, mv2_done, rstd2_done)

            root1((0, 0))
            pool.wait_ge(const_loaded, 16 * 5)
            bias_rows((0, 0))
            root1((0, 1))

            def low_part(e, slot, i):
                pool.wait_ge(high_done, CHUNKS * e + i + 1)
                w, high, low = chunk(slot, i)
                pool.tensor_tensor(low, w, high.bitcast(fp32), ALU.subtract).then_inc(low_done, 1)

            def stage(e):
                pool.wait_ge(low_done, CHUNKS * e)
                stand(pool)
                pool.dma_start(st1[:, :, :], w1[ds(e, 1), :, :].rearrange("e (c p) n -> p (e c) n", p=128))\
                    .then_inc(stage_loaded, 16)
                pool.dma_start(st2[:, :, :], w2[ds(e, 1), :, :].rearrange("e (c p) n -> p (e c) n", p=128))\
                    .then_inc(stage_loaded, 16)

            def normalise(g, c):
                n = KC * num(g) + c
                pool.wait_ge(weight_done, n + 1)
                wait(pool, prT_mm, QUADS // KC * (n - 1))
                pool.tensor_tensor(pr[:, c, :, :, :], ex[:, c, :, :].unsqueeze(2).broadcast_to([P, HB, NB, T]),
                                   weight[:, c, :, :].unsqueeze(3).broadcast_to([P, HB, NB, T]), ALU.mult)\
                    .then_inc(pr_done, 1)

            def scatter(g):
                pool.wait_ge(dest_done, num(g) + 1)
                pool.wait_ge(row1_done, num(g) + 1)
                stand(pool)
                for k in range(K):
                    pool.indirect_dma_start(dispatch, bass.IndirectOffsetOnAxis(ap=dest[:, g[1], k:k + 1], axis=0),
                                            rows[:, g[1], k, :], None).then_inc(scattered[g[1]], 16)

            def step(g):
                if exists(by(g, 2)):
                    root1(by(g, 2))
                if exists(g):
                    normalise(g, 0)
                if exists(g):
                    normalise(g, 1)
                if exists(by(g, 1)):
                    bias_rows(by(g, 1))
                if exists(by(g, -1)):
                    root2(by(g, -1))
                if exists(by(g, -2)):
                    scatter(by(g, -2))
                if isinstance(g[0], int) and num(g) < CHUNKS:
                    low_part(0, 0, num(g))
                if isinstance(g[0], int) and num(g) == CHUNKS - 1:
                    stage(1)

            over_groups(pool, step)

            pool.sem_inc(y_free, ONE)
            for r in (0, 1):
                pool.wait_ge(h2_stored[r], 16 * PAIRS)

            def tiles(e):
                first_e = load_table(pool, first_i, e)
                last_e = load_table(pool, first_i, e + 1)
                with pool.Fori(first_e, last_e) as t:
                    for half in (0, 1):
                        pool.wait_ge(y_ready, ONE + 2 * t + half + 1)
                        stand(pool)
                        pool.indirect_dma_start(out, bass.IndirectOffsetOnAxis(ap=y_dest[:, half:half + 1], axis=0),
                                                y[:, half, :], None, compute_op=ALU.add).then_inc(y_added, 16)
                    pool.wait_ge(y_added, 32 * t + 32)
                    pool.sem_inc(y_free, 1)

            with pool.Fori(0, E // 2 - 1) as pair:
                for r in (0, 1):
                    e = 2 * pair + r
                    for i in range(CHUNKS):
                        low_part(e + 1, 1 - r, i)
                    stage(e + 2)
                    tiles(e)
            for i in range(CHUNKS):
                low_part(E - 1, 1, i)
            tiles(E - 2)
            tiles(E - 1)

        @block.scalar
        def _(act):
            act.dma_start(vec_rows[0:E * HC, :], b1.rearrange("e (j p) -> (e j) p", p=128)).then_inc(const_loaded, 16)
            act.dma_start(vec_rows[E * HC:E * HC + KC, :], bq.rearrange("(c p) -> c p", p=128)).then_inc(const_loaded, 16)
            act.dma_start(bk_row[:, :], bk.rearrange("(a n) -> a n", a=1)).then_inc(const_loaded, 16)
            act.dma_start(bv_bc[:, :], bv.partition_broadcast(P)).then_inc(const_loaded, 16)
            act.dma_start(bo_bc[:, :], bo.partition_broadcast(P)).then_inc(const_loaded, 16)

            def h_out(g):
                n = num(g)
                act.wait_ge(h_mm, n + 1)
                wait(act, hbo_done, n - 1)
                wait(act, xn_done, n - 1)
                act.activation(h_sb[:, g[1], :], ps_h[0:P, 0:D], ACT.Copy).then_inc(h_done, 1)

            def xTs_out(a, b):
                act.wait_ge(xTs_mm, num(a) + 1)
                cols = slice(0 if exists(a) else KC, 2 * KC if exists(b) else KC)
                act.activation(xTs[:, cols, :].rearrange("p c n -> p (c n)"), ps_xv[:, cols.start * P:cols.stop * P],
                               ACT.Copy).then_inc(xTs_done, 1)

            def exp(g, c):
                n = KC * num(g) + c
                act.wait_ge(sm_done, n + 1)
                wait(act, pr_done, n + 1 - KC)
                act.activation(ex[:, c, :, :], sm[:, c, :, :], ACT.Exp).then_inc(exp_done, 1)

            def queries_out(g):
                act.wait_ge(kq_mm, num(g) + 1)
                for c in range(KC):
                    last = act.activation(qT[:, g[1], c, :].rearrange("p (b s) -> p b s", b=NB)[:, :, 0:T],
                                          ps_kq[:, (KC + c) * P:(KC + c + 1) * P].rearrange("p (b t) -> p b t", b=NB),
                                          ACT.Identity, bias=bq_q[:, c:c + 1], scale=float(HD) ** -0.5)
                last.then_inc(q_done, 1)

            def keys_out(g):
                for h in range(HB):
                    last = act.activation(kT[:, g[1], :, h, :], ps_kq[:, 0:KC * P].rearrange("p (c k) -> p c k", c=KC),
                                          ACT.Copy, scale=in_head[:, h:h + 1])
                last.then_inc(k_done, 1)

            def high_part(e, slot, i):
                w, high, low = chunk(slot, i)
                act.activation(high, w, ACT.Copy).then_inc(high_done, 1)

            def second_row(g):
                act.wait_ge(row0_done, num(g) + 1)
                act.activation(rows[:, g[1], 1, 0:D], rows[:, g[1], 0, 0:D], ACT.Copy).then_inc(row1_done, 1)

            def probT_out(g, q):
                n = QUADS * num(g) + q
                act.wait_ge(prT_mm, n + 1)
                wait(act, cxT_mm, num(g))
                act.activation(prT[:, q * QH:(q + 1) * QH, :].rearrange("p h k -> p (h k)"),
                               ps_probT[q % 2][0:P, 0:QH * P], ACT.Copy).then_inc(prT_done, 1)

            def ctxT_out(g):
                act.wait_ge(cxT_mm, num(g) + 1)
                act.activation(cxT[:, :, :].rearrange("p c n -> p (c n)"), ps_ctx[:, 0:KC * P], ACT.Copy)\
                    .then_inc(cxT_done, 1)

            def gate_exp(g):
                act.wait_ge(top_done, num(g) + 1)
                act.activation(gexp[:, :], top[:, 0:K], ACT.Exp, bias=neg_top[:, 0:1],
                               accum_out=gsum[:, 0:1]).then_inc(gexp_done, 1)

            h_out((0, 0))
            xTs_out((0, 0), (-2, 1))
            act.wait_ge(setup_done, 1)
            queries_out((0, 0))
            keys_out((0, 0))
            h_out((0, 1))

            def step(g):
                context, routed = exists(by(g, -1)), exists(by(g, -2))
                if context:
                    probT_out(by(g, -1), 0)
                    probT_out(by(g, -1), 1)
                if exists(by(g, 2)):
                    h_out(by(g, 2))
                if exists(by(g, 1)) or routed:
                    xTs_out(by(g, 1), by(g, -2))
                if exists(g):
                    exp(g, 0)
                if context:
                    probT_out(by(g, -1), 2)
                if exists(g):
                    exp(g, 1)
                if context:
                    probT_out(by(g, -1), 3)
                if routed:
                    second_row(by(g, -2))
                if exists(by(g, 1)):
                    queries_out(by(g, 1))
                if context:
                    ctxT_out(by(g, -1))
                if exists(by(g, 1)):
                    keys_out(by(g, 1))
                if routed:
                    gate_exp(by(g, -2))
                if isinstance(g[0], int) and num(g) < CHUNKS:
                    act.wait_ge(stage0_loaded, 32)
                    high_part(0, 0, num(g))

            over_groups(act, step)

            act.wait_ge(tables_done, 1)

            def round_rows(n):
                act.wait_ge(xr_mm, ONE + n)
                act.activation(xh[:, :, :].rearrange("p c n -> p (c n)"), ps_xT[:, :], ACT.Copy).then_inc(xh_done, 1)

            act.sem_inc(hf_done, ONE)
            round_rows(1)

            def tile(e, t, slot, opens):
                for b in range(4):
                    act.wait_ge(hid_mm, 4 * t + b + 1)
                    for j in (2 * b, 2 * b + 1):
                        last = act.activation(hf[:, j, :], ps_hidden[b][:, (j % 2) * TILE:(j % 2 + 1) * TILE], ACT.Relu,
                                              bias=b1_cur[:, j:j + 1])
                    last.then_inc(hf_done, 1)
                    if opens and b == 0:
                        act.wait_ge(stage_loaded, 32 * (e + 1))
                    if opens and b < 2:
                        high_part(e + 1, 1 - slot, b)
                round_rows(t + 2)
                if opens:
                    high_part(e + 1, 1 - slot, 2)
                    high_part(e + 1, 1 - slot, 3)

            def expert(e, slot, more):
                first_e = load_table(act, first_i, e)
                act.wait_ge(hf_done, ONE + 4 * first_e)
                act.activation(b1_cur[:, :], b1_cols[:, ds(HC * e, HC)], ACT.Copy).then_inc(act_b1, 1)
                act.wait_ge(act_b1, e + 1)
                last_e = load_table(act, first_i, e + 1)
                tile(e, first_e, slot, more)
                with act.Fori(first_e + 1, last_e) as t:
                    tile(e, t, slot, False)

            with act.Fori(0, E // 2 - 1) as pair:
                for slot in (0, 1):
                    expert(2 * pair + slot, slot, True)
            expert(E - 2, 0, True)
            expert(E - 1, 1, False)

        @block.vector
        def _(dve):
            done = [0]

            def link(ins):
                done[0] += 1
                ins.then_inc(dve_order, 1)
                dve.wait_ge(dve_order, done[0])

            dve.wait_ge(iotas_made, 1)
            dve.wait_ge(taps_loaded, 16)
            for tap_i, hit, n in ((tap1_i, hit1, N_IN), (tap2_i, hit2, T)):
                last = dve.scalar_tensor_tensor(hit[:, :, :], tap_i[:, :, :], 0.0,
                                                h0_bc[0:N_MID, :].unsqueeze(1).broadcast_to([N_MID, n, TAPS]),
                                                ALU.is_equal, ALU.mult)
            link(last)
            dve.tensor_reduce(level1[:, :], hit1[:, :, :], X, ALU.add)
            link(dve.tensor_reduce(level2[:, :], hit2[:, :, :], X, ALU.add))
            dve.sem_inc(levels_made, 1)
            dve.wait_ge(masks_made, 1)
            dve.wait_ge(wave_mm, 1)
            for b in range(NB):
                last = dve.tensor_copy(wave[:, b, b * T:(b + 1) * T], ps_kq[0:N_IN, 0:T])
            last.then_inc(wave_made, 1)
            dve.wait_ge(iotas_made, 2)
            dve.tensor_copy(rel[:, :], rel_i[:, :])
            dve.tensor_copy(part[:, :], part_i[:, :])
            dve.tensor_copy(experts[:, :], experts_i[:, :])
            dve.tensor_copy(steps[:, :], steps_i[:, :])
            dve.tensor_scalar(later[:, :, :], later_i[:, :, :], 0.0, None, ALU.is_gt)
            link(dve.tensor_scalar(strip_i[:, :], part_i[:, :], HD.bit_length() - 1, None, ALU.logical_shift_right))
            dve.tensor_copy(in_head[:, :], heads_i[:, :])
            for b in range(NB + 1):
                dve.tensor_scalar(reached[:, b:b + 1], part[0:P, :], float(b * T), None, ALU.is_ge)
            link(dve.tensor_copy(strip[:, :], strip_i[:, :]))
            for b in range(1, NB):
                link(dve.scalar_tensor_tensor(rel[:, :], reached[:, b:b + 1].broadcast_to([P, T]), float(T), rel[:, :],
                                              ALU.mult, ALU.add))
            dve.tensor_tensor(own[:, :], reached[:, 0:NB], reached[:, 1:NB + 1], ALU.subtract)
            dve.tensor_scalar(in_head[:, :], in_head[:, :], strip[:, 0:1], None, ALU.is_equal)
            root = (2.0 ** 8) ** (1.0 / HEADS)
            for h in range(HEADS):
                dve.tensor_scalar(score_bias[:, h, :], rel[:, :], 1.0 / root ** (h + 1), None, ALU.mult)
            dve.tensor_scalar(region[:, :], experts[:, :], float(REGION), None, ALU.mult)
            dve.tensor_scalar(live[:, :], part[:, :], float(LAST_BATCHES * T), None, ALU.is_lt)
            dve.tensor_scalar(dead[:, :], part[:, :], float(LAST_BATCHES * T), None, ALU.is_ge)
            for k in range(K):
                last = dve.tensor_scalar(spill[:, k:k + 1], part[:, :], float(SPILL + HALF * k), None, ALU.add)
            link(last)
            dve.tensor_scalar(spill[:, :], spill[:, :], dead[:, 0:1], None, ALU.mult)
            dve.wait_ge(masks_made, 3)
            for half in (0, 1):
                dve.tensor_scalar(pad_rows[:, half, D:D + 1].bitcast(i32), part[:, :], float(PAD_ROW + half * HALF), None,
                                  ALU.add)
            dve.tensor_copy(token[:, :], part[:, :])
            link(dve.memset(count[:, :], 0.0))
            dve.wait_ge(vec_mm, 1)
            link(dve.tensor_copy(vec_cols[:, :], ps_ctx[:, 0:E * HC + KC]))
            link(dve.tensor_scalar(bq_q[:, :], bq_cols, float(HD) ** -0.5, None, ALU.mult))
            dve.sem_inc(setup_done, 1)
            FIRST, LINKS = 4, 12
            links, at = [0, 0], [None]

            def glink(ins):
                if isinstance(at[0][0], int):
                    link(ins)
                else:
                    links[1] += 1
                    ins.then_inc(dve_order, 1)
                    dve.wait_ge(dve_order, links[0] + LINKS * (num(at[0]) - FIRST) + links[1])

            def moments1(g):
                dve.wait_ge(h_done, num(g) + 1)
                glink(dve.bn_stats(stats[:, :], h_sb[:, g[1], :]))
                stand(dve)
                dve.bn_aggr(mv[:, :], stats[:, :]).then_inc(mv_done, 1)

            def norm1(g):
                dve.wait_ge(rstd_done, num(g) + 1)
                wait(dve, xTs_mm, num(g))
                dve.tensor_scalar(xn[:, :], h_sb[:, g[1], :], mv[:, 0:1], rstd[:, 0:1], ALU.subtract, ALU.mult)\
                    .then_inc(xn_done, 1)

            def values_out(g):
                n, r = num(g), g[1]
                dve.wait_ge(v_mm, n + 1)
                wait(dve, cxT_mm, n - 1)
                for odd_head in (0, 1):
                    last = dve.tensor_tensor(va[:, r, :, 2 * odd_head, :],
                                             ps_xv[0:P, 0:D].rearrange("p (j o d) -> p j o d", o=2, d=HD)[:, :, odd_head, :],
                                             bv_bc[:, :].rearrange("p (j o d) -> p j o d", o=2, d=HD)[:, :, odd_head, :],
                                             ALU.add)
                last.then_inc(v_done, 1)

            def scores(g, c):
                n = KC * num(g) + c
                dve.wait_ge(s_mm, n + 1)
                dve.tensor_tensor(sc[:, c, :, :], ps_scores[c][0:P, 0:HB * T].rearrange("p (h k) -> p h k", h=HB),
                                  score_bias[:, c * HB:(c + 1) * HB, :], ALU.add).then_inc(sc_done, 1)
                dve.wait_ge(sc_done, n + 1)
                dve.tensor_reduce(mx[:, c, :], sc[:, c, :, :], X, ALU.max).then_inc(mx_done, 1)
                dve.wait_ge(mx_done, n + 1)
                wait(dve, exp_done, n + 1 - KC)
                dve.tensor_tensor(sm[:, c, :, :], sc[:, c, :, :], mx[:, c, :].unsqueeze(2).broadcast_to([P, HB, T]),
                                  ALU.subtract).then_inc(sm_done, 1)

            def weights(g, c):
                n = KC * num(g) + c
                dve.wait_ge(exp_done, n + 1)
                dve.tensor_reduce(pr_sum[:, c, :], ex[:, c, :, :], X, ALU.add).then_inc(psum_done, 1)
                dve.wait_ge(psum_done, n + 1)
                dve.reciprocal(rsum[:, c, :], pr_sum[:, c, :]).then_inc(rsum_done, 1)
                dve.wait_ge(rsum_done, n + 1)
                wait(dve, pr_done, n + 1 - KC)
                dve.tensor_tensor(weight[:, c, :, :], rsum[:, c, :].unsqueeze(2).broadcast_to([P, HB, NB]),
                                  own[:, :].unsqueeze(1).broadcast_to([P, HB, NB]), ALU.mult).then_inc(weight_done, 1)

            def moments2(g):
                n = num(g)
                r = g[1]
                dve.wait_ge(wo_mm, n + 1)
                dve.wait_ge(hbo_done, n + 1)
                wait(dve, h2_stored[r], 16 * g[0])
                dve.tensor_tensor(h2[:, r, :], ps_ctx[0:P, D:2 * D], hbo[:, r, :], ALU.add).then_inc(h2_done, 1)
                dve.wait_ge(h2_done, n + 1)
                glink(dve.bn_stats(stats2[:, :], h2[:, r, :]))
                stand(dve)
                dve.bn_aggr(mv2[:, :], stats2[:, :]).then_inc(mv2_done, 1)

            def norm2(g):
                dve.wait_ge(rstd2_done, num(g) + 1)
                wait(dve, scattered[g[1]], 16 * K * g[0])
                dve.tensor_scalar(rows[:, g[1], 0, 0:D], h2[:, g[1], :], mv2[:, 0:1], rstd2[:, 0:1],
                                  ALU.subtract, ALU.mult).then_inc(row0_done, 1)

            def choose(g):
                n = num(g)
                dve.wait_ge(lg_mm, n + 1)
                glink(dve.tensor_copy(lg[:, :], ps_scores[0][0:P, LG]))
                stand(dve)
                glink(dve.max(top[:, :], lg[:, :]))
                dve.tensor_scalar(neg_top[:, :], top[:, 0:1], -1.0, None, ALU.mult).then_inc(top_done, 1)
                if not (isinstance(g[0], int) and n == 0):
                    dve.tensor_scalar(token[:, :], token[:, :], float(P), None, ALU.add)
                glink(dve.max_index(top_i[:, :], top[:, :], lg[:, :]))
                glink(dve.tensor_copy(choice[:, :], top_i[:, 0:K]))
                glink(dve.tensor_tensor(hot[:, :, :], experts[0:P, :].unsqueeze(1).broadcast_to([P, K, E]),
                                        choice[:, :].unsqueeze(2).broadcast_to([P, K, E]), ALU.is_equal))
                if is_last(g):
                    link_last(dve.tensor_scalar(hot[:, :, :], hot[:, :, :], live[0:P, 0:1], None, ALU.mult))
                dve.tensor_tensor(hot_any[:, :], hot[:, 0, :], hot[:, 1, :], ALU.add).then_inc(hot_done, 1)

            last_links = [0]
            last_order = sem("last_order")

            def link_last(ins):
                last_links[0] += 1
                ins.then_inc(last_order, 1)
                dve.wait_ge(last_order, last_links[0])

            def place(g, between):
                n = num(g)
                r = g[1]
                dve.wait_ge(rank_mm, n + 1)
                glink(dve.tensor_tensor(pos_all[:, :], ps_scores[1][0:P, RANK], count[0:P, :], ALU.add))
                dve.tensor_tensor(count[:, :], ps_scores[1][:, COUNT], count[:, :], ALU.add).then_inc(rank_read, 1)
                glink(dve.tensor_tensor(pos_hot[:, :, :], hot[:, :, :], pos_all[:, :].unsqueeze(1).broadcast_to([P, K, E]),
                                        ALU.mult))
                glink(dve.tensor_reduce(pos[:, :], pos_hot[:, :, :], X, ALU.add))
                dve.wait_ge(gexp_done, n + 1)
                dve.reciprocal(grec[:, :], gsum[:, :])
                dve.tensor_scalar(keep[:, :], pos[:, :], float(CAP), None, ALU.is_lt)
                glink(dve.scalar_tensor_tensor(dest_f[:, :], choice[:, :], float(REGION), pos[:, :], ALU.mult, ALU.add))
                between()
                if is_last(g):
                    link_last(dve.tensor_scalar(dest_f[:, :], dest_f[:, :], live[0:P, 0:1], None, ALU.mult))
                    link_last(dve.tensor_scalar(keep[:, :], keep[:, :], live[0:P, 0:1], None, ALU.mult))
                    link_last(dve.tensor_tensor(dest_f[:, :], dest_f[:, :], spill[0:P, :], ALU.add))
                dve.tensor_copy(dest[:, r, :], dest_f[:, :])
                glink(dve.tensor_scalar(gate[:, :], gexp[:, :], grec[:, 0:1], None, ALU.mult))
                dve.tensor_tensor(rows[:, r, :, D + 1], gate[:, :], keep[:, :], ALU.mult)
                for k in range(K):
                    last = dve.tensor_copy(rows[:, r, k, D:D + 1].bitcast(i32), token[0:P, :])
                last.then_inc(dest_done, 1)

            at[0] = (0, 0)
            moments1((0, 0))
            norm1((0, 0))
            values_out((0, 0))
            moments1((0, 1))
            norm1((0, 1))

            def step(g):
                if isinstance(at[0][0], int):
                    links[0] = done[0]
                at[0], links[1] = g, 0
                if exists(by(g, 2)):
                    moments1(by(g, 2))
                if exists(g):
                    scores(g, 0)
                    scores(g, 1)
                    weights(g, 0)
                    weights(g, 1)
                if exists(by(g, -2)):
                    choose(by(g, -2))
                if exists(by(g, 2)):
                    norm1(by(g, 2))
                if exists(by(g, 1)):
                    values_out(by(g, 1))
                if exists(by(g, -1)):
                    moments2(by(g, -1))
                normed = [not exists(by(g, -1))]

                def norm2_once():
                    if not normed[0]:
                        norm2(by(g, -1))
                    normed[0] = True

                if exists(by(g, -2)):
                    place(by(g, -2), norm2_once)
                norm2_once()
                if not isinstance(g[0], int):
                    assert links[1] == LINKS
                    done[0] = links[0] + LINKS * (GROUPS - 2 - FIRST)

            over_groups(dve, step)

            dve.wait_ge(rank_read, GROUPS)
            dve.tensor_tensor(pad_row[:, :], count[:, :], region[:, :], ALU.add)
            link(dve.tensor_tensor(full[:, :, :], count[:, :].unsqueeze(2).broadcast_to([128, E, 2 * MAXT]),
                                   steps[:, :].unsqueeze(1).broadcast_to([128, E, 2 * MAXT]), ALU.is_gt))
            dve.tensor_copy(pad_row_i[:, :], pad_row[:, :])
            dve.tensor_reduce(nhalves[:, :], full[:, :, :], X, ALU.add)
            link(dve.tensor_reduce(ntiles[:, :], full[:, :, 0:2 * MAXT:2], X, ALU.add))
            dve.memset(end[:, 0:1], 0.0)
            dve.tensor_scalar(nhalves[:, :], nhalves[:, :], 1.0, None, ALU.max)
            link(dve.tensor_scalar(ntiles[:, :], ntiles[:, :], 1.0, None, ALU.max))
            link(dve.tensor_tensor(before_e[:, :, :], later[:, :, :], ntiles[:, :].unsqueeze(1).broadcast_to([128, E + 1, E]),
                                   ALU.mult))
            link(dve.tensor_reduce(first[:, :], before_e[:, :, :], X, ALU.add))
            dve.tensor_copy(first_i[:, :], first[:, :])
            dve.scalar_tensor_tensor(end[:, 1:E + 1], first[:, 0:E], 2.0, nhalves[:, :], ALU.mult, ALU.add)
            link(dve.scalar_tensor_tensor(origin[:, :], first[:, 0:E], -float(TILE), region[:, :], ALU.mult, ALU.add))
            dve.tensor_copy(end_i[:, :], end[:, :])
            link(dve.tensor_copy(origin_i[:, :], origin[:, :]))
            dve.sem_inc(tables_done, 1)

            def split_rows(t):
                dve.wait_ge(xr_loaded, 16 * (t + 1))
                wait(dve, meta_kept, t)
                dve.tensor_copy(meta_next[:, :, :], xr[:, :, D:ROW]).then_inc(meta_taken, 1)
                dve.wait_ge(xh_done, t + 1)
                dve.tensor_tensor(xl[:, :, :].rearrange("p c n -> p (c n)"), ps_xT[:, :],
                                  xh[:, :, :].bitcast(fp32).rearrange("p c n -> p (c n)"), ALU.subtract).then_inc(xs_done, 1)

            for s in (meta_taken, y_read, y_ready):
                dve.sem_inc(s, ONE)
            split_rows(0)
            dve.wait_ge(b2_loaded, 16)
            with dve.Fori(0, E) as e:
                first_e = load_table(dve, first_i, e)
                dve.wait_ge(y_read, ONE + 2 * first_e)
                dve.tensor_copy(b2_cur[:, :], b2_bc[:, ds(e, 1), :].rearrange("p e d -> p (e d)"))
                last_e = load_table(dve, first_i, e + 1)
                with dve.Fori(first_e, last_e) as t:
                    dve.wait_ge(y_ready, ONE + 2 * t)
                    dve.wait_ge(meta_taken, ONE + t + 1)
                    dve.tensor_copy(meta[:, :, :], meta_next[:, :, :]).then_inc(meta_kept, 1)
                    for b in range(4):
                        dve.wait_ge(hf_done, ONE + 4 * t + b + 1)
                        dve.tensor_copy(hh[:, 2 * b:2 * b + 2, :], hf[:, 2 * b:2 * b + 2, :]).then_inc(hh_done, 1)
                        dve.wait_ge(hh_done, 4 * t + b + 1)
                        dve.tensor_tensor(hl[:, 2 * b:2 * b + 2, :], hf[:, 2 * b:2 * b + 2, :],
                                          hh[:, 2 * b:2 * b + 2, :].bitcast(fp32), ALU.subtract).then_inc(hs_done, 1)
                    split_rows(t + 1)
                    dve.wait_ge(y_mm, ONE + t + 1)
                    for half in (0, 1):
                        n = 2 * t + half
                        dve.tensor_tensor(yb[:, half, :], ps_y[half][:, 0:D], b2_cur[:, :], ALU.add).then_inc(y_read, 1)
                        dve.wait_ge(y_free, ONE + t)
                        dve.wait_ge(y_read, ONE + n + 1)
                        dve.tensor_copy(y_dest[:, half:half + 1], meta[:, half, 0:1].bitcast(i32))
                        dve.tensor_scalar(y[:, half, :], yb[:, half, :], meta[:, half, 1:2], None, ALU.mult)\
                            .then_inc(y_ready, 1)

        @block.tensor
        def _(pe):
            def transposes(dst, src, rows_, cols):
                for c in range(KC):
                    last = pe.transpose(dst[:, c * cols:(c + 1) * cols], src[:, c * 128:(c + 1) * 128],
                                        ident[0:rows_, 0:rows_])
                return last

            pe.wait_ge(levels_made, 1)
            pe.matmul(ps_kq[0:N_IN, 0:T], level1[:, :], level2[:, :], start=True, stop=True).then_inc(wave_mm, 1)

            def wavelet(g):
                r = g[1]
                pe.wait_ge(x_loaded[r], 16 * (g[0] + 1))
                wait(pe, h_done, num(g))
                for b in range(NB):
                    last = pe.matmul(ps_h[0:P, 0:D], wave[:, b, :], x_sb[:, r, b * D:(b + 1) * D],
                                     start=(b == 0), stop=(b == NB - 1))
                last.then_inc(h_mm, 1)

            def norms_T(a, b):
                if exists(a):
                    pe.wait_ge(xn_done, num(a) + 1)
                wait(pe, v_done, up_to(num(a), GROUPS))
                if exists(a):
                    last = transposes(ps_xv, xn, P, P)
                if exists(b):
                    pe.wait_ge(row0_done, num(b) + 1)
                    last = transposes(ps_xv[:, KC * P:2 * KC * P], rows[:, b[1], 0, :], P, P)
                last.then_inc(xTs_mm, 1)

            def queries_keys(g):
                pe.wait_ge(xTs_done, num(g) + 1)
                wait(pe, k_done, num(g))
                for m in range(KC):
                    for c in range(KC):
                        pe.matmul(ps_kq[:, (KC + m) * P:(KC + m + 1) * P], wq_sb[:, c, m * 128:(m + 1) * 128], xT[:, c, :],
                                  start=(c == 0), stop=(c == KC - 1))
                for m in range(KC):
                    for c in range(KC):
                        pe.matmul(ps_kq[:, m * P:(m + 1) * P], wk_sb[:, c, m * 128:(m + 1) * 128], xT[:, c, :],
                                  start=(c == 0), stop=False)
                    last = pe.matmul(ps_kq[:, m * P:(m + 1) * P], bk_row[:, m * 128:(m + 1) * 128], ones[0:1, 0:P],
                                     start=False, stop=True)
                last.then_inc(kq_mm, 1)

            def project_values(g):
                for c in range(KC):
                    last = pe.matmul(ps_xv[0:P, 0:D], xT[:, c, :], wv_sb[:, c, :], start=(c == 0), stop=(c == KC - 1))
                last.then_inc(v_mm, 1)

            def scores(g, c):
                n = KC * num(g) + c
                pe.wait_ge(q_done, num(g) + 1)
                pe.wait_ge(k_done, num(g) + 1)
                wait(pe, sc_done, n + 1 - KC)
                wait(pe, (top_done, rank_read)[c], num(g) - 2)
                for b in range(NB):
                    last = pe.matmul(ps_scores[c][0:P, 0:HB * T], qT[:, g[1], c, b * P:(b + 1) * P],
                                     kT[:, g[1], c, :, b * T:(b + 1) * T], start=(b == 0), stop=(b == NB - 1))
                last.then_inc(s_mm, 1)

            def prob_T(g, q):
                n = QUADS * num(g) + q
                c = q // (QUADS // KC)
                pe.wait_ge(pr_done, KC * num(g) + c + 1)
                wait(pe, prT_done, n - 1)
                for i in range(QH):
                    last = pe.transpose(ps_probT[q % 2][0:P, i * P:(i + 1) * P],
                                        pr[:, c, (q * QH + i) % HB, :, :].rearrange("p b k -> p (b k)"),
                                        ident[0:P, 0:P])
                last.then_inc(prT_mm, 1)

            def attend(g):
                pe.wait_ge(prT_done, QUADS * num(g) + QUADS)
                pe.wait_ge(v_done, num(g) + 1)
                wait(pe, cxT_done, num(g))
                wait(pe, h2_done, num(g))
                for c in range(KC):
                    for odd_head in (0, 1):
                        for j in range(HPAIRS // KC):
                            pair_ = HPAIRS // KC * c + j
                            last = pe.matmul(ps_ctx[32 * j:32 * j + 32, c * P:(c + 1) * P],
                                             va[:, g[1], pair_, odd_head:odd_head + 2, :].rearrange("p z d -> p (z d)"),
                                             prT[:, 2 * pair_ + odd_head, :], start=(odd_head == 0), stop=(odd_head == 1))
                last.then_inc(cxT_mm, 1)

            def project(g):
                pe.wait_ge(cxT_done, num(g) + 1)
                for c in range(KC):
                    last = pe.matmul(ps_ctx[0:P, D:2 * D], cxT[:, c, :], wo_sb[:, c, :], start=(c == 0), stop=(c == KC - 1))
                last.then_inc(wo_mm, 1)

            def route(g):
                pe.wait_ge(xTs_done, num(g) + 4)
                pe.wait_ge(sc_done, up_to(KC * (num(g) + 2) + 1, KC * GROUPS))
                for c in range(KC):
                    last = pe.matmul(ps_scores[0][0:P, LG], x2T[:, c, :], wr_sb[:, c, :], start=(c == 0), stop=(c == KC - 1))
                last.then_inc(lg_mm, 1)

            def rank(g):
                pe.wait_ge(hot_done, num(g) + 1)
                pe.wait_ge(sc_done, up_to(KC * (num(g) + 2) + 2, KC * GROUPS))
                pe.matmul(ps_scores[1][0:P, RANK], before[:, :], hot_any[:, :], start=True, stop=True)
                pe.matmul(ps_scores[1][:, COUNT], ones[:, :], hot_any[:, :], start=True, stop=True).then_inc(rank_mm, 1)

            pe.wait_ge(wave_made, 1)
            wavelet((0, 0))
            pe.wait_ge(masks_made, 4)
            pe.wait_ge(const_loaded, 16 * 5)
            n_vec = E * HC + KC
            pe.transpose(ps_ctx[:, 0:n_vec], vec_rows[0:n_vec, :], ident[0:n_vec, 0:n_vec]).then_inc(vec_mm, 1)
            pe.wait_ge(proj_loaded, 16 * 5)
            norms_T((0, 0), (-2, 1))
            pe.wait_ge(setup_done, 1)
            queries_keys((0, 0))
            project_values((0, 0))
            wavelet((0, 1))

            def step(g):
                context, routed = exists(by(g, -1)), exists(by(g, -2))
                if context:
                    prob_T(by(g, -1), 0)
                    prob_T(by(g, -1), 1)
                if exists(by(g, 2)):
                    wavelet(by(g, 2))
                if exists(g):
                    scores(g, 0)
                if exists(by(g, 1)) or routed:
                    norms_T(by(g, 1), by(g, -2))
                if exists(g):
                    scores(g, 1)
                if context:
                    prob_T(by(g, -1), 2)
                    prob_T(by(g, -1), 3)
                if routed:
                    route(by(g, -2))
                if exists(by(g, 1)):
                    queries_keys(by(g, 1))
                if context:
                    attend(by(g, -1))
                if exists(by(g, 1)):
                    project_values(by(g, 1))
                if context:
                    project(by(g, -1))
                if routed:
                    rank(by(g, -2))

            over_groups(pe, step)

            pe.wait_ge(tables_done, 1)

            def row_T(n):
                pe.wait_ge(xr_loaded, 16 * n)
                for c in range(KC):
                    for half in (0, 1):
                        last = pe.transpose(ps_xT[:, c * TILE + half * HALF:c * TILE + (half + 1) * HALF],
                                            xr[:, half, c * 128:(c + 1) * 128], ident[:, :])
                last.then_inc(xr_mm, 1)

            for s in (xr_mm, y_mm):
                pe.sem_inc(s, ONE)
            row_T(1)
            with pe.Fori(0, E // 2) as pair:
                _, ends = nc.values_load_multi_w_load_instructions(end_i[0:1, ds(2 * pair, 3)], engines=(mybir.EngineType.PE,),
                                                                   min_val=0, max_val=E * REGION)
                starts = [(end + 1) // 2 for end in ends]
                for slot in (0, 1):
                    pe.wait_ge(low_done, CHUNKS * (2 * pair + slot + 1))
                    stand(pe)
                    with pe.Fori(starts[slot], starts[slot + 1]) as t:
                        pe.wait_ge(xs_done, t + 1)
                        for b in range(4):
                            for j in (2 * b, 2 * b + 1):
                                js = slice(j * 128, (j + 1) * 128)
                                terms = [(w, v, c) for c in range(KC)
                                         for w, v in ((w1h, xh), (w1h, xl), (w1l, xh))]
                                for i, (w, v, c) in enumerate(terms):
                                    last = pe.matmul(ps_hidden[b][:, (j % 2) * TILE:(j % 2 + 1) * TILE], w[:, slot, c, js],
                                                     v[:, c, :], start=(i == 0), stop=(i == len(terms) - 1))
                            last.then_inc(hid_mm, 1)
                        row_T(t + 2)
                        pe.wait_ge(y_read, ONE + 2 * t)

                        def output(half):
                            hs = slice(half * HALF, (half + 1) * HALF)
                            for j in range(HC):
                                if j % 2 == 0:
                                    pe.wait_ge(hs_done, 4 * t + j // 2 + 1)
                                for i, (v, w) in enumerate(((hh, w2h), (hh, w2l), (hl, w2h))):
                                    last = pe.matmul(ps_y[half][:, 0:D], v[:, j, hs], w[:, slot, j, :],
                                                     start=(j == 0 and i == 0), stop=(j == HC - 1 and i == 2))
                            return last

                        with pe.If(2 * t + 1 < ends[slot + 1]):
                            output(1)
                        output(0).then_inc(y_mm, 1)


_INS = ['x', 'L0_tok_h0', 'L0_attn_Wq', 'L0_attn_bq', 'L0_attn_Wk', 'L0_attn_bk', 'L0_attn_Wv', 'L0_attn_bv',
        'L0_attn_Wo', 'L0_attn_bo', 'L0_ffn_w_router', 'L0_ffn_w1', 'L0_ffn_b1', 'L0_ffn_w2', 'L0_ffn_b2']


def kernel(**inputs):
    import numpy as _np
    import concourse.bacc as _bacc
    from concourse import mybir as _mybir
    from concourse.bass_utils import run_bass_kernel_spmd as _run

    nc = _bacc.Bacc("TRN2", target_bir_lowering=False, num_devices=1)
    arrays, args = {}, []
    for name in _INS:
        a = _np.ascontiguousarray(inputs[name])
        arrays[f"in_{name}"] = a
        args.append(nc.dram_tensor(f"in_{name}", a.shape, _mybir.dt.from_np(a.dtype), kind="ExternalInput").ap())
    args.append(nc.dram_tensor("out_rows", (OUT_ROWS, D), _mybir.dt.float32, kind="ExternalOutput").ap())
    audio_tower(nc, *args)
    r = _run(nc, [arrays], core_ids=[0])
    return _np.asarray(r.results[0]["out_rows"])[0:TOKENS].reshape(B, T, D)
```
